# Optimizing a Trainium2 kernel written in Bass

```python
import numpy as np
import jax
import jax.numpy as jnp

def _softmax(x, axis=-1):
    return jax.nn.softmax(x, axis=axis)

def _gelu(x):
    return jax.nn.gelu(x, approximate=True)

def _silu(x):
    return jax.nn.silu(x)

def _sigmoid(x):
    return jax.nn.sigmoid(x)

def _layernorm(x, axis=-1, eps=1e-05):
    m = jnp.mean(x, axis=axis, keepdims=True)
    v = jnp.var(x, axis=axis, keepdims=True)
    return (x - m) / jnp.sqrt(v + eps)

def _scatter_add(tgt, idx, src, axis=0):
    return tgt.at[idx].add(src)

def _segment_sum(src, seg, n):
    return jax.ops.segment_sum(src, seg, n)
kernel_name = 'mk_vit_tower_d1_tok_img512_r4_a89534'

def setup_inputs(seed: int=0):
    np.random.seed(seed)
    _w = jnp.asarray

    def _rec_inputs():
        import jax
        import jax.numpy as jnp
        _rk = jax.random.key(seed)
        x = -0.000356955 + 1 * jax.random.normal(jax.random.fold_in(_rk, 1), (16, 3, 128, 128), jnp.float32)
        return x
    x = _rec_inputs()

    def _L0_tok_setup():
        import jax, jax.numpy as jnp
        import numpy as np
        key = jax.random.key(seed)
        k1, k2, k3 = jax.random.split(key, 3)
        B, C, H, W = (128, 3, 224, 224)
        E, p = (128, 16)
        K = C * p * p
        img = jax.random.normal(k1, (B, C, H, W), dtype=jnp.float32)
        w = jax.random.normal(k2, (E, K), dtype=jnp.float32) * (1.0 / np.sqrt(K))
        b = jax.random.normal(k3, (E,), dtype=jnp.float32)
        return {'img': img, 'w': w, 'b': b, 'patch_size': p}
    _L0_tok_all = _L0_tok_setup()
    _L0_tok_in = {k: v for k, v in _L0_tok_all.items() if k in ('w', 'b')}
    del _L0_tok_all

    def _L0_attn_setup():
        import jax, jax.numpy as jnp
        import numpy as np
        EMBED = 128
        HEADS = 8
        HD = EMBED // HEADS // 2
        EXP = 4
        DEPTH = 1
        LAMBDA_INIT = 0.8 - 0.6 * float(np.exp(-0.3 * (DEPTH - 1)))
        EPS = 1e-05

        def layernorm(x, w, b):
            mu = jnp.mean(x, axis=-1, keepdims=True)
            var = jnp.mean(jnp.square(x - mu), axis=-1, keepdims=True)
            return (x - mu) * jax.lax.rsqrt(var + EPS) * w + b

        def rmsnorm(x, w):
            ms = jnp.mean(jnp.square(x), axis=-1, keepdims=True)
            return x * jax.lax.rsqrt(ms + EPS) * w

        def diff_attn(x, Wq, Wk, Wv, Wo, lq1, lk1, lq2, lk2, subln_w):
            B, N, D = x.shape
            q = (x @ Wq.T).reshape(B, N, 2 * HEADS, HD).transpose(0, 2, 1, 3)
            k = (x @ Wk.T).reshape(B, N, 2 * HEADS, HD).transpose(0, 2, 1, 3)
            v = (x @ Wv.T).reshape(B, N, HEADS, 2 * HD).transpose(0, 2, 1, 3)
            q = q * HD ** (-0.5)
            scores = jnp.einsum('bhnd,bhmd->bhnm', q, k)
            attn = jax.nn.softmax(scores, axis=-1)
            attn = attn.reshape(B, HEADS, 2, N, N)
            lam1 = jnp.exp(jnp.sum(lq1 * lk1))
            lam2 = jnp.exp(jnp.sum(lq2 * lk2))
            lam = lam1 - lam2 + LAMBDA_INIT
            attn = attn[:, :, 0] - lam * attn[:, :, 1]
            out = jnp.einsum('bhnm,bhmd->bhnd', attn, v)
            out = rmsnorm(out, subln_w) * (1.0 - LAMBDA_INIT)
            out = out.transpose(0, 2, 1, 3).reshape(B, N, D)
            return out @ Wo.T
        key = jax.random.key(seed)
        ks = jax.random.split(key, 12)
        B, N, D = (8, 256, EMBED)
        s = 0.02
        inp = {'x': jax.random.normal(ks[0], (B, N, D), jnp.float32), 'Wq': jax.random.normal(ks[1], (D, D), jnp.float32) * s, 'Wk': jax.random.normal(ks[2], (D, D), jnp.float32) * s, 'Wv': jax.random.normal(ks[3], (D, D), jnp.float32) * s, 'Wo': jax.random.normal(ks[4], (D, D), jnp.float32) * s, 'lq1': jax.random.normal(ks[5], (HD,), jnp.float32) * 0.1, 'lk1': jax.random.normal(ks[6], (HD,), jnp.float32) * 0.1, 'lq2': jax.random.normal(ks[7], (HD,), jnp.float32) * 0.1, 'lk2': jax.random.normal(ks[8], (HD,), jnp.float32) * 0.1, 'subln_w': jnp.ones((2 * HD,), jnp.float32), 'n1_w': jnp.ones((D,), jnp.float32), 'n1_b': jnp.zeros((D,), jnp.float32), 'n2_w': jnp.ones((D,), jnp.float32), 'n2_b': jnp.zeros((D,), jnp.float32), 'mln1_w': jnp.ones((D,), jnp.float32), 'mln1_b': jnp.zeros((D,), jnp.float32), 'mW1': jax.random.normal(ks[9], (EXP * D, D), jnp.float32) * s, 'mb1': jnp.zeros((EXP * D,), jnp.float32), 'mln2_w': jnp.ones((EXP * D,), jnp.float32), 'mln2_b': jnp.zeros((EXP * D,), jnp.float32), 'mW2': jax.random.normal(ks[10], (D, EXP * D), jnp.float32) * s, 'mb2': jnp.zeros((D,), jnp.float32)}
        return inp
    _L0_attn_all = _L0_attn_setup()
    _L0_attn_in = {k: v for k, v in _L0_attn_all.items() if k in ('Wq', 'Wk', 'Wv', 'Wo', 'lq1', 'lk1', 'lq2', 'lk2', 'subln_w', 'n1_w', 'n1_b', 'n2_w', 'n2_b', 'mln1_w', 'mln1_b', 'mW1', 'mb1', 'mln2_w', 'mln2_b', 'mW2', 'mb2')}
    del _L0_attn_all

    def _L0_ffn_setup():
        import jax, jax.numpy as jnp
        import numpy as np
        MICRO_BATCHES = 2
        TOP_K = 2
        D = 128
        E = 8
        B, S = (8, 2048)
        key = jax.random.key(seed)
        ks = jax.random.split(key, 12)
        s = 0.02
        return {'x': jax.random.normal(ks[0], (B, S, D), dtype=jnp.float32), 'ln_g': jnp.ones((D,), jnp.float32), 'ln_b': jnp.zeros((D,), jnp.float32), 'attn_w': jax.random.normal(ks[1], (D, D), jnp.float32) * s, 'attn_b': jnp.zeros((D,), jnp.float32), 'gate_w': jax.random.normal(ks[2], (E, D), jnp.float32) * s, 'fc1_w': jax.random.normal(ks[3], (E, 4 * D, D), jnp.float32) * s, 'fc1_b': jnp.zeros((E, 4 * D), jnp.float32), 'fc2_w': jax.random.normal(ks[4], (E, D, 4 * D), jnp.float32) * s, 'fc2_b': jnp.zeros((E, D), jnp.float32), 'next_w': jax.random.normal(ks[5], (D, D), jnp.float32) * s, 'next_b': jnp.zeros((D,), jnp.float32)}
    _L0_ffn_all = _L0_ffn_setup()
    _L0_ffn_in = {k: v for k, v in _L0_ffn_all.items() if k in ('ln_g', 'ln_b', 'attn_w', 'attn_b', 'gate_w', 'fc1_w', 'fc1_b', 'fc2_w', 'fc2_b', 'next_w', 'next_b')}
    del _L0_ffn_all
    return {'x': x, 'L0_tok_w': _L0_tok_in['w'], 'L0_tok_b': _L0_tok_in['b'], 'L0_attn_Wq': _L0_attn_in['Wq'], 'L0_attn_Wk': _L0_attn_in['Wk'], 'L0_attn_Wv': _L0_attn_in['Wv'], 'L0_attn_Wo': _L0_attn_in['Wo'], 'L0_attn_lq1': _L0_attn_in['lq1'], 'L0_attn_lk1': _L0_attn_in['lk1'], 'L0_attn_lq2': _L0_attn_in['lq2'], 'L0_attn_lk2': _L0_attn_in['lk2'], 'L0_attn_subln_w': _L0_attn_in['subln_w'], 'L0_attn_n1_w': _L0_attn_in['n1_w'], 'L0_attn_n1_b': _L0_attn_in['n1_b'], 'L0_attn_n2_w': _L0_attn_in['n2_w'], 'L0_attn_n2_b': _L0_attn_in['n2_b'], 'L0_attn_mln1_w': _L0_attn_in['mln1_w'], 'L0_attn_mln1_b': _L0_attn_in['mln1_b'], 'L0_attn_mW1': _L0_attn_in['mW1'], 'L0_attn_mb1': _L0_attn_in['mb1'], 'L0_attn_mln2_w': _L0_attn_in['mln2_w'], 'L0_attn_mln2_b': _L0_attn_in['mln2_b'], 'L0_attn_mW2': _L0_attn_in['mW2'], 'L0_attn_mb2': _L0_attn_in['mb2'], 'L0_ffn_ln_g': _L0_ffn_in['ln_g'], 'L0_ffn_ln_b': _L0_ffn_in['ln_b'], 'L0_ffn_attn_w': _L0_ffn_in['attn_w'], 'L0_ffn_attn_b': _L0_ffn_in['attn_b'], 'L0_ffn_gate_w': _L0_ffn_in['gate_w'], 'L0_ffn_fc1_w': _L0_ffn_in['fc1_w'], 'L0_ffn_fc1_b': _L0_ffn_in['fc1_b'], 'L0_ffn_fc2_w': _L0_ffn_in['fc2_w'], 'L0_ffn_fc2_b': _L0_ffn_in['fc2_b'], 'L0_ffn_next_w': _L0_ffn_in['next_w'], 'L0_ffn_next_b': _L0_ffn_in['next_b']}

def reference(x, L0_tok_w, L0_tok_b, L0_attn_Wq, L0_attn_Wk, L0_attn_Wv, L0_attn_Wo, L0_attn_lq1, L0_attn_lk1, L0_attn_lq2, L0_attn_lk2, L0_attn_subln_w, L0_attn_n1_w, L0_attn_n1_b, L0_attn_n2_w, L0_attn_n2_b, L0_attn_mln1_w, L0_attn_mln1_b, L0_attn_mW1, L0_attn_mb1, L0_attn_mln2_w, L0_attn_mln2_b, L0_attn_mW2, L0_attn_mb2, L0_ffn_ln_g, L0_ffn_ln_b, L0_ffn_attn_w, L0_ffn_attn_b, L0_ffn_gate_w, L0_ffn_fc1_w, L0_ffn_fc1_b, L0_ffn_fc2_w, L0_ffn_fc2_b, L0_ffn_next_w, L0_ffn_next_b):
    import jax
    import jax.numpy as jnp

    def _L0_tok_ref(img, w, b, patch_size):
        import jax, jax.numpy as jnp
        import numpy as np
        B, C, H, W = img.shape
        p = patch_size
        Hp, Wp = (H // p, W // p)
        S = Hp * Wp
        patches = img.reshape(B, C, Hp, p, Wp, p)
        patches = patches.transpose(0, 2, 4, 1, 3, 5).reshape(B, S, C * p * p)
        out = jnp.einsum('bsk,ek->bse', patches, w) + b
        return out

    def _L0_attn_ref(x, Wq, Wk, Wv, Wo, lq1, lk1, lq2, lk2, subln_w, n1_w, n1_b, n2_w, n2_b, mln1_w, mln1_b, mW1, mb1, mln2_w, mln2_b, mW2, mb2):
        import jax, jax.numpy as jnp
        import numpy as np
        EMBED = 128
        HEADS = 8
        HD = EMBED // HEADS // 2
        EXP = 4
        DEPTH = 1
        LAMBDA_INIT = 0.8 - 0.6 * float(np.exp(-0.3 * (DEPTH - 1)))
        EPS = 1e-05

        def layernorm(x, w, b):
            mu = jnp.mean(x, axis=-1, keepdims=True)
            var = jnp.mean(jnp.square(x - mu), axis=-1, keepdims=True)
            return (x - mu) * jax.lax.rsqrt(var + EPS) * w + b

        def rmsnorm(x, w):
            ms = jnp.mean(jnp.square(x), axis=-1, keepdims=True)
            return x * jax.lax.rsqrt(ms + EPS) * w

        def diff_attn(x, Wq, Wk, Wv, Wo, lq1, lk1, lq2, lk2, subln_w):
            B, N, D = x.shape
            q = (x @ Wq.T).reshape(B, N, 2 * HEADS, HD).transpose(0, 2, 1, 3)
            k = (x @ Wk.T).reshape(B, N, 2 * HEADS, HD).transpose(0, 2, 1, 3)
            v = (x @ Wv.T).reshape(B, N, HEADS, 2 * HD).transpose(0, 2, 1, 3)
            q = q * HD ** (-0.5)
            scores = jnp.einsum('bhnd,bhmd->bhnm', q, k)
            attn = jax.nn.softmax(scores, axis=-1)
            attn = attn.reshape(B, HEADS, 2, N, N)
            lam1 = jnp.exp(jnp.sum(lq1 * lk1))
            lam2 = jnp.exp(jnp.sum(lq2 * lk2))
            lam = lam1 - lam2 + LAMBDA_INIT
            attn = attn[:, :, 0] - lam * attn[:, :, 1]
            out = jnp.einsum('bhnm,bhmd->bhnd', attn, v)
            out = rmsnorm(out, subln_w) * (1.0 - LAMBDA_INIT)
            out = out.transpose(0, 2, 1, 3).reshape(B, N, D)
            return out @ Wo.T
        x_res = x
        xn = layernorm(x, n1_w, n1_b)
        a = diff_attn(xn, Wq, Wk, Wv, Wo, lq1, lk1, lq2, lk2, subln_w)
        h = layernorm(a, n2_w, n2_b) + x_res
        z = layernorm(h, mln1_w, mln1_b)
        z = jax.nn.gelu(z @ mW1.T + mb1, approximate=False)
        z = layernorm(z, mln2_w, mln2_b)
        z = z @ mW2.T + mb2
        return z + h

    def _L0_ffn_ref(x, ln_g, ln_b, attn_w, attn_b, gate_w, fc1_w, fc1_b, fc2_w, fc2_b, next_w, next_b):
        import jax, jax.numpy as jnp
        import numpy as np
        MICRO_BATCHES = 2
        TOP_K = 2
        D = 128
        E = 8
        B, S = (8, 2048)
        b, s, d = x.shape
        xf = x.reshape(b * s, d)
        mu = jnp.mean(xf, axis=-1, keepdims=True)
        var = jnp.var(xf, axis=-1, keepdims=True)
        normed = (xf - mu) / jnp.sqrt(var + 1e-05) * ln_g + ln_b
        x_attn = normed @ attn_w.T + attn_b + xf
        logits = x_attn @ gate_w.T
        _scores, _indices = jax.lax.top_k(logits, TOP_K)
        e = fc1_w.shape[0]
        t = b * s // (MICRO_BATCHES * e)
        tok = x_attn.reshape(MICRO_BATCHES, e, t, d)
        h = jnp.einsum('meti,ehi->meth', tok, fc1_w) + fc1_b[None, :, None, :]
        h = jax.nn.gelu(h, approximate=False)
        y = jnp.einsum('meth,edh->metd', h, fc2_w) + fc2_b[None, :, None, :]
        yf = y.reshape(b * s, d)
        out = jax.nn.gelu(yf @ next_w.T + next_b, approximate=False)
        return out.reshape(b, s, d)
    h = _L0_tok_ref(x, L0_tok_w, L0_tok_b, 16)
    h = h + _L0_attn_ref(_layernorm(h, axis=-1), L0_attn_Wq, L0_attn_Wk, L0_attn_Wv, L0_attn_Wo, L0_attn_lq1, L0_attn_lk1, L0_attn_lq2, L0_attn_lk2, L0_attn_subln_w, L0_attn_n1_w, L0_attn_n1_b, L0_attn_n2_w, L0_attn_n2_b, L0_attn_mln1_w, L0_attn_mln1_b, L0_attn_mW1, L0_attn_mb1, L0_attn_mln2_w, L0_attn_mln2_b, L0_attn_mW2, L0_attn_mb2)
    h = h + _L0_ffn_ref(_layernorm(h, axis=-1), L0_ffn_ln_g, L0_ffn_ln_b, L0_ffn_attn_w, L0_ffn_attn_b, L0_ffn_gate_w, L0_ffn_fc1_w, L0_ffn_fc1_b, L0_ffn_fc2_w, L0_ffn_fc2_b, L0_ffn_next_w, L0_ffn_next_b)
    return h

_drawn_inputs = setup_inputs


def setup_inputs(seed=0):
    import zlib

    import numpy as np

    out = dict(_drawn_inputs(seed))
    spreads = {'L0_attn_subln_w': (1.0, 0.2),
     'L0_attn_n1_w': (1.0, 0.2),
     'L0_attn_n1_b': (0.0, 0.1),
     'L0_attn_n2_w': (1.0, 0.2),
     'L0_attn_n2_b': (0.0, 0.1),
     'L0_attn_mln1_w': (1.0, 0.6),
     'L0_attn_mln1_b': (0.0, 0.462),
     'L0_attn_mb1': (0.0, 0.1),
     'L0_attn_mln2_w': (1.0, 0.552),
     'L0_attn_mln2_b': (0.0, 0.423),
     'L0_attn_mb2': (0.0, 0.1),
     'L0_ffn_ln_g': (1.0, 0.6),
     'L0_ffn_ln_b': (0.0, 0.8),
     'L0_ffn_attn_b': (0.0, 0.8),
     'L0_ffn_fc1_b': (0.0, 0.8),
     'L0_ffn_fc2_b': (0.0, 0.8),
     'L0_ffn_next_b': (0.0, 2.0)}
    factors = {'L0_attn_Wq': 8.0,
     'L0_attn_Wk': 8.0,
     'L0_attn_lq1': 8.0,
     'L0_attn_lk1': 8.0,
     'L0_attn_lq2': 8.0,
     'L0_attn_lk2': 8.0,
     'L0_ffn_attn_w': 8.0,
     'L0_ffn_fc1_w': 8.0,
     'L0_ffn_fc2_w': 8.0,
     'L0_ffn_next_w': 8.0}
    for name, (base, spread) in spreads.items():
        noise = np.random.default_rng([zlib.crc32(name.encode()), seed]).standard_normal(out[name].shape)
        drawn = base * np.exp(spread * noise) if base else spread * noise
        out[name] = jnp.asarray(drawn.astype(out[name].dtype))
    for name, factor in factors.items():
        out[name] = (out[name] * factor).astype(out[name].dtype)
    return out
```

```python
import concourse.bass as bass
from concourse import mybir
from contextlib import ExitStack

P = 128
TILES = 8
G = 2
TG = TILES // G
COLS = TG * P
KC = 6
HEADS = 8
HD = 8
NB = 2
N = 64
SUB = 2 * HEADS
VC = 2 * HD + 1
OH = 128
HC = 4
HID = HC * P
EPS = 1e-5
LAMBDA_INIT = 0.8 - 0.6 * 1.0

COL = {}
for _name, _n in (("n1_w", 1), ("n1_b", 1), ("subln_w", 1), ("mln1_w", 1), ("mln1_b", 1), ("mln2_w", HC),
                  ("mln2_b", HC), ("ln_g", 1), ("ln_b", 1), ("attn_b", 1), ("fc1_b", TILES * HC),
                  ("fc2_b", TILES)):
    COL[_name] = sum(n for _, n in COL.values()), _n
NCOL = sum(n for _, n in COL.values())
ROW = {}
for _name, _n in (("tok_b", P), ("n2_w", P), ("n2_b", P), ("mb2", P), ("next_b", P), ("mb1", HID), ("lam", 4 * HD)):
    ROW[_name] = sum(n for _, n in ROW.values()), _n
NROW = sum(n for _, n in ROW.values())


def vit_layer(nc, xT, tok_wT, cols, rows, qkvoT, w1T, w2T, attnT, nextT, fc1T, fc2T, out):
    fp32 = mybir.dt.float32
    ALU = mybir.AluOpType
    ACT = mybir.ActivationFunctionType
    AX = mybir.AxisListType.X

    ctx = ExitStack()
    with ctx:
        def sb(name, shape):
            return ctx.enter_context(nc.sbuf_tensor(name, shape, fp32))

        def sem(name):
            return ctx.enter_context(nc.semaphore(name))

        x_sb = sb("x_sb", [P, G, KC, COLS])
        tokw = sb("tokw", [P, KC, P])
        col_sb = sb("col_sb", [P, NCOL])
        row_sb = sb("row_sb", [P, NROW])
        qkvo = sb("qkvo", [P, 4, P])
        w1 = sb("w1", [P, HID])
        w2 = sb("w2", [P, HC, P])
        wattn = sb("wattn", [P, P])
        wnext = sb("wnext", [P, P])
        fc1 = sb("fc1", [P, TILES, HID])
        fc2 = sb("fc2", [P, TILES, HC, P])
        ident = sb("ident", [P, P])
        exponent = sb("exponent", [P, TG * HEADS])
        sub_scale = sb("sub_scale", [P, 1])
        lam_prod = sb("lam_prod", [P, 2, HD])
        lam_dot = sb("lam_dot", [P, 2])
        lam_exp = sb("lam_exp", [P, 2])
        lam_diff = sb("lam_diff", [P, 1])
        neg_lam = sb("neg_lam", [P, 1])
        h0 = sb("h0", [P, TILES, P])
        xin = sb("xin", [P, TILES, P])
        cent = sb("cent", [P, TILES, P])
        attn = sb("attn", [P, TILES, HEADS, 2 * HD])
        tmp = sb("tmp", [P, TILES, P])
        h = sb("h", [P, TILES, P])
        hsum = sb("hsum", [P, TILES, P])
        h1 = sb("h1", [P, TILES, P])
        hid = sb("hid", [P, TILES, HID])
        xnT = sb("xnT", [P, G, COLS])
        qT = sb("qT", [P, G, COLS])
        kT = sb("kT", [P, G, COLS])
        hidT = x_sb[:, 0, 0:HC]
        kdiag = sb("kdiag", [P, G * TG * NB, SUB // 2, N])
        vdiag = sb("vdiag", [P, TILES * NB, HEADS, 2, VC])
        prob = sb("prob", [P, 2, SUB, N])
        probT = sb("probT", [P, 2, HEADS, P])
        negmax = sb("negmax", [P, 2, SUB])
        rden = sb("rden", [P, 2, HEADS, 2])
        onorm = sb("onorm", [P, 2, HEADS, 2, 2 * HD])
        stats = sb("stats", [P, TG, 6])
        mv = sb("mv", [P, 5, G, TG, 2])
        var = sb("var", [P, 6, G, TG * HEADS])
        rstd = sb("rstd", [P, 6, G, TG * HEADS])

        pairs = [ctx.enter_context(nc.psum_tensor(f"banks{2 * i}{2 * i + 1}", [P, 2 * COLS], fp32)) for i in range(4)]

        def bank(i):
            return pairs[i // 2][:, (i % 2) * COLS:(i % 2 + 1) * COLS]

        def col(name, i=0):
            at = COL[name][0] + i
            return col_sb[:, at:at + 1]

        def row(name, tiles):
            at, n = ROW[name]
            return row_sb[:, at:at + n][:, None, :].to_broadcast([P, tiles, n])

        def tiled(ap):
            return ap.rearrange("p (t n) -> p t n", n=P)

        def of_group(t, g):
            return t[:, g * TG:(g + 1) * TG]

        s_tokw, s_col, s_row, s_qkvo = sem("tokw_in"), sem("cols_in"), sem("rows_in"), sem("qkvo_in")
        s_x = [[sem(f"x_in_{g}_{c}") for c in range(KC)] for g in range(G)]
        s_w1, s_w2, s_wan = sem("w1_in"), sem("w2_in"), sem("wattn_wnext_in")
        s_fc1 = [sem(f"fc1_in_{e}") for e in range(TILES)]
        s_fc2 = [sem(f"fc2_in_{e}") for e in range(TILES)]
        s_ident0, s_ident, s_half, s_zero = sem("ident_cleared"), sem("ident_ready"), sem("exponent_ready"), sem("diags_cleared")
        s_ones = sem("ones_ready")
        s_lamdot, s_lamexp, s_lam, s_subs = sem("lam_dots"), sem("lam_exps"), sem("lam_ready"), sem("sub_scale_ready")
        s_dve, s_act, s_pool = sem("vector_steps"), sem("scalar_steps"), sem("pool_steps")
        s_var = [sem(f"var_ready_{k}") for k in range(6)]
        s_rstd = [sem(f"rstd_ready_{k}") for k in range(6)]
        s_kdiag = [sem(f"kdiag_ready_{g}") for g in range(G)]
        names = ("tok_done h0_ready xin_ready xc_ready xcT_done xnT_ready q_done qT_ready k_done kT_ready "
                 "v_done vdiag_ready s_done shifted exp_done probT_done probT_ready o_done o_read rms_ready aT_done "
                 "aT_ready wo_done wo_read h_ready hsum_ready zc_ready zcT_done zT_ready w1_done w1_read gelu_ready hidn_ready "
                 "hidT_done hidT_ready w2_done h1_ready n_ready nT_done nT_ready xa_done xaT_ready fc1_done "
                 "fgelu_ready fc2_done yT_ready next_done next_read ngelu_ready out_ready stored").split()
        S = {n: sem(n) for n in names}

        block = ctx.enter_context(nc.Block())

        @block.sync
        def _(sp):
            sp.dma_start(tokw[:], tok_wT.rearrange("c p e -> p c e")).then_inc(s_tokw, 16)
            for c in range(KC):
                sp.dma_start(x_sb[:, 0, c], xT[0, c]).then_inc(s_x[0][c], 16)
            sp.dma_start(row_sb[:], rows.to_broadcast([P, NROW])).then_inc(s_row, 16)
            sp.dma_start(col_sb[:], cols).then_inc(s_col, 16)
            sp.dma_start(qkvo[:], qkvoT).then_inc(s_qkvo, 16)
            for c in range(KC):
                sp.dma_start(x_sb[:, 1, c], xT[1, c]).then_inc(s_x[1][c], 16)

            def spread_k(g):
                sp.wait_ge(s_zero, 1)
                sp.wait_ge(S["kT_ready"], g + 1)
                for s in range(SUB):
                    rows8 = slice(s * HD, (s + 1) * HD)
                    at = g * TG * NB
                    sp.dma_start(kdiag[rows8, at:at + TG * NB, s % (SUB // 2), :],
                                 kT[rows8, g].rearrange("p (b n) -> p b n", n=N)).then_inc(s_kdiag[g], 16)

            spread_k(0)
            sp.dma_start(w1[:], w1T).then_inc(s_w1, 16)
            spread_k(1)
            sp.dma_start(w2[:], w2T.rearrange("c p n -> p c n")).then_inc(s_w2, 16)
            sp.dma_start(wattn[:], attnT).then_inc(s_wan, 16)
            sp.dma_start(wnext[:], nextT).then_inc(s_wan, 16)
            for e in range(TILES):
                sp.dma_start(fc1[:, e], fc1T[e]).then_inc(s_fc1[e], 16)
                sp.dma_start(fc2[:, e], fc2T[e]).then_inc(s_fc2[e], 16)
            for g in range(G):
                sp.wait_ge(S["out_ready"], g + 1)
                sp.dma_start(out[g], of_group(tmp, g)).then_inc(S["stored"], 16)
            sp.wait_ge(S["stored"], 16 * G)

        @block.gpsimd
        def _(pool):
            nc.gpsimd.memset(exponent[:], -0.5).then_inc(s_half, 1)
            nc.gpsimd.memset(ident[:], 0.0).then_inc(s_ident0, 1)
            pool.wait_ge(s_ident0, 1)
            nc.gpsimd.affine_select(out=ident[:], in_=ident[:], compare_op=ALU.not_equal, fill=1.0, base=0,
                                    pattern=[[-1, P]], channel_multiplier=1).then_inc(s_ident, 1)
            nc.gpsimd.memset(kdiag[:], 0.0).then_inc(s_zero, 1)
            nc.gpsimd.memset(vdiag[:], 0.0).then_inc(s_zero, 1)
            pool.wait_ge(s_zero, 2)
            for j in range(2):
                nc.gpsimd.memset(vdiag[j * N:(j + 1) * N, :, :, j, 2 * HD:VC], 1.0).then_inc(s_ones, 1)
                pool.wait_ge(s_ones, j + 1)
            pool.wait_ge(s_half, 1)

            def inverse_root(k, g, n):
                pool.wait_ge(s_var[k], g + 1)
                nc.gpsimd.tensor_tensor(rstd[:, k, g, 0:n], var[:, k, g, 0:n], exponent[:, 0:n], ALU.pow)\
                  .then_inc(s_rstd[k], 1)

            for g in range(G):
                inverse_root(0, g, 2 * TG)
            for k, n in ((1, TG * HEADS), (2, TG), (3, TG), (4, TG), (5, 2 * TG)):
                for g in range(G):
                    inverse_root(k, g, n)

        @block.scalar
        def _(act):
            def affine(dst, src, w, b):
                return nc.scalar.activation(dst, src, ACT.Identity, scale=w, bias=b)

            act.wait_ge(s_lamdot, 1)
            nc.scalar.activation(lam_exp[:], lam_dot[:], ACT.Exp).then_inc(s_lamexp, 1)
            act.wait_ge(s_col, 16)
            nc.scalar.activation(sub_scale[:], col("subln_w"), ACT.Copy, scale=1.0 - LAMBDA_INIT).then_inc(s_subs, 1)

            def input_norm(g):
                act.wait_ge(S["xcT_done"], g + 1)
                affine(xnT[:, g], bank(2 + g), col("n1_w"), col("n1_b")).then_inc(S["xnT_ready"], 1)

            def projections(g):
                act.wait_ge(S["k_done"], g + 1)
                nc.scalar.activation(kT[:, g], bank(5), ACT.Copy).then_inc(S["kT_ready"], 1)
                act.wait_ge(S["q_done"], g + 1)
                nc.scalar.activation(qT[:, g], bank(4), ACT.Copy, scale=HD ** -0.5).then_inc(S["qT_ready"], 1)

            def exponentials(t):
                act.wait_ge(S["shifted"], t + 1)
                nc.scalar.activation(prob[:, t % 2], prob[:, t % 2], ACT.Exp).then_inc(S["exp_done"], 1)

            def transposed_probs(t):
                act.wait_ge(S["probT_done"], t + 1)
                if t >= 2:
                    act.wait_ge(S["o_done"], t - 1)
                nc.scalar.activation(probT[:, t % 2].rearrange("p h n -> p (h n)"), pairs[2][:, :], ACT.Copy)\
                  .then_inc(S["probT_ready"], 1)

            def attention_out(g):
                act.wait_ge(s_subs, 1)
                act.wait_ge(S["aT_done"], g + 1)
                nc.scalar.activation(xnT[:, g], bank(g), ACT.Copy, scale=sub_scale[:]).then_inc(S["aT_ready"], 1)

            def mlp_in(g):
                act.wait_ge(S["zcT_done"], g + 1)
                affine(qT[:, g], bank(4 + g), col("mln1_w"), col("mln1_b")).then_inc(S["zT_ready"], 1)

            def mlp_gelu(g):
                for t in range(g * TG, (g + 1) * TG):
                    act.wait_ge(S["w1_read"], t + 1)
                    nc.scalar.activation(hid[:, t], hid[:, t], ACT.Gelu).then_inc(S["gelu_ready"], 1)

            def mlp_hidden(g):
                for c in range(HC):
                    act.wait_ge(S["hidT_done"], g * HC + c + 1)
                    if g > 0:
                        act.wait_ge(S["w2_done"], g)
                    affine(hidT[:, c], bank(c), col("mln2_w", c), col("mln2_b", c)).then_inc(S["hidT_ready"], 1)

            def ffn_in(g):
                act.wait_ge(S["nT_done"], g + 1)
                affine(xnT[:, g], bank(6), col("ln_g"), col("ln_b")).then_inc(S["nT_ready"], 1)

            def ffn_tokens(g):
                act.wait_ge(S["xa_done"], g + 1)
                nc.scalar.activation(qT[:, g], bank(7), ACT.Identity, bias=col("attn_b")).then_inc(S["xaT_ready"], 1)

            def expert_gelu(g):
                for e in range(g * TG, (g + 1) * TG):
                    act.wait_ge(S["fc1_done"], e + 1)
                    for c in range(HC):
                        part = slice(c * P, (c + 1) * P)
                        ins = nc.scalar.activation(hid[:, e, part], bank(e % 4)[:, part], ACT.Gelu,
                                                   bias=col("fc1_b", e * HC + c))
                    ins.then_inc(S["fgelu_ready"], 1)

            def last_gelu(g):
                act.wait_ge(S["next_read"], g + 1)
                part = of_group(tmp, g)
                nc.scalar.activation(part, part, ACT.Gelu).then_inc(S["ngelu_ready"], 1)

            for g in range(G):
                input_norm(g)
                projections(g)
            exponentials(0)
            for t in range(TILES):
                transposed_probs(t)
                if t + 1 < TILES:
                    exponentials(t + 1)
            for stage in (attention_out, mlp_in, mlp_gelu, mlp_hidden):
                for g in range(G):
                    stage(g)
            for g in range(G):
                ffn_in(g)
                ffn_tokens(g)
            for stage in (expert_gelu, last_gelu):
                for g in range(G):
                    stage(g)

        @block.vector
        def _(dve):
            steps = [0]

            def step(ins):
                steps[0] += 1
                ins.then_inc(s_dve, 1)
                return steps[0]

            def settle():
                dve.wait_ge(s_dve, steps[0])

            def moments(k, g, src):
                for t in range(TG):
                    step(nc.vector.bn_stats(stats[:, t], src[:, t]))
                settle()
                for t in range(TG):
                    step(nc.vector.bn_aggr(mv[:, k, g, t], stats[:, t]))
                settle()

            def shifted_variance(k, norm, g):
                nc.vector.tensor_scalar(var[:, norm, g, 0:TG], mv[:, k, g, :, 1], EPS, None, ALU.add)\
                  .then_inc(s_var[norm], 1)

            def double_variance(k, norm, g):
                step(nc.vector.tensor_scalar(var[:, norm, g, 0:TG], mv[:, k, g, :, 1], EPS, None, ALU.add))
                settle()
                nc.vector.tensor_scalar(var[:, norm, g, TG:2 * TG], mv[:, k, g, :, 1], 1.0 + EPS, EPS * EPS,
                                        ALU.mult, ALU.add).then_inc(s_var[norm], 1)

            def normalise(dst, src, k, norm, g, second=0):
                for t in range(TG):
                    ins = nc.vector.tensor_scalar(dst[:, t], src[:, t], mv[:, k, g, t, 0:1],
                                                  rstd[:, norm, g, second * TG + t:second * TG + t + 1],
                                                  ALU.subtract, ALU.mult)
                return ins

            def add(dst, a, b):
                return nc.vector.tensor_tensor(dst, a, b, ALU.add)

            dve.wait_ge(s_row, 16)
            lam = row_sb[:, ROW["lam"][0]:NROW].rearrange("p (a b d) -> p a b d", a=2, b=2)
            step(nc.vector.tensor_tensor(lam_prod[:], lam[:, :, 0], lam[:, :, 1], ALU.mult))
            settle()
            nc.vector.tensor_reduce(lam_dot[:], lam_prod[:], AX, ALU.add).then_inc(s_lamdot, 1)
            dve.wait_ge(s_lamexp, 1)
            step(nc.vector.tensor_tensor(lam_diff[:], lam_exp[:, 1:2], lam_exp[:, 0:1], ALU.subtract))
            settle()
            step(nc.vector.tensor_scalar(neg_lam[:], lam_diff[:], -LAMBDA_INIT, None, ALU.add))
            settle()

            def embedding(g):
                dve.wait_ge(S["tok_done"], g + 1)
                add(of_group(h0, g), tiled(bank(g)), row("tok_b", TG)).then_inc(S["h0_ready"], 1)
                dve.wait_ge(S["h0_ready"], g + 1)
                moments(0, g, of_group(h0, g))
                double_variance(0, 0, g)

            def input_norm(g):
                dve.wait_ge(s_rstd[0], g + 1)
                normalise(of_group(cent, g), of_group(h0, g), 0, 0, g, second=1).then_inc(S["xc_ready"], 1)
                step(normalise(of_group(xin, g), of_group(h0, g), 0, 0, g))

            def values(g):
                if g == 0:
                    dve.wait_ge(s_zero, 2)
                for i in range(2):
                    dve.wait_ge(S["v_done"], 2 * g + i + 1)
                    src = bank(6 + i).rearrange("p (b h d) -> p b h d", h=HEADS, d=2 * HD)
                    at = g * TG * NB + 4 * i
                    for j in range(2):
                        half = slice(j * N, (j + 1) * N)
                        ins = nc.vector.tensor_copy(vdiag[half, at:at + 4, :, j, 0:2 * HD], src[half])
                    ins.then_inc(S["vdiag_ready"], 1)

            def softmax_shift(t):
                dve.wait_ge(S["s_done"], t + 1)
                scores = pairs[t % 2][:, :].rearrange("p (s n) -> p s n", n=N)
                step(nc.vector.tensor_reduce(negmax[:, t % 2], scores, AX, ALU.max, negate=True))
                settle()
                if t >= 2:
                    dve.wait_ge(S["probT_done"], t - 1)
                add(prob[:, t % 2], scores, negmax[:, t % 2][:, :, None].to_broadcast([P, SUB, N]))\
                    .then_inc(S["shifted"], 1)

            def difference(t):
                dve.wait_ge(S["o_done"], t + 1)
                o = pairs[3][:, :].rearrange("p (h x) -> p h x", x=OH)[:, :, 0:2 * NB * VC]\
                    .rearrange("p h (b j c) -> p h b j c", b=NB, j=2)
                for b in range(NB):
                    half = slice(b * N, (b + 1) * N)
                    step(nc.vector.reciprocal(rden[half, t % 2], o[half, :, b, :, 2 * HD]))
                settle()
                step(nc.vector.tensor_scalar(rden[:, t % 2, :, 1], rden[:, t % 2, :, 1], neg_lam[:], None, ALU.mult))
                settle()
                for b in range(NB):
                    half = slice(b * N, (b + 1) * N)
                    ins = nc.vector.tensor_tensor(onorm[half, t % 2], o[half, :, b, :, 0:2 * HD],
                                                  rden[half, t % 2][:, :, :, None].to_broadcast([N, HEADS, 2, 2 * HD]),
                                                  ALU.mult)
                ins.then_inc(S["o_read"], 1)
                dve.wait_ge(S["o_read"], t + 1)
                step(add(attn[:, t], onorm[:, t % 2, :, 0], onorm[:, t % 2, :, 1]))

            def rms(g):
                settle()
                a = of_group(attn, g).rearrange("p t h d -> p (t h) d")
                sq = of_group(tmp, g).rearrange("p t (h d) -> p (t h) d", d=2 * HD)
                step(nc.vector.tensor_tensor(sq, a, a, ALU.mult))
                settle()
                step(nc.vector.tensor_reduce(var[:, 1, g], sq, AX, ALU.add))
                settle()
                nc.vector.tensor_scalar(var[:, 1, g], var[:, 1, g], 1.0 / (2 * HD), EPS, ALU.mult, ALU.add)\
                  .then_inc(s_var[1], 1)

            def rms_apply(g):
                dve.wait_ge(s_rstd[1], g + 1)
                a = of_group(attn, g).rearrange("p t h d -> p (t h) d")
                nc.vector.tensor_tensor(of_group(cent, g).rearrange("p t (h d) -> p (t h) d", d=2 * HD), a,
                                        rstd[:, 1, g][:, :, None].to_broadcast([P, TG * HEADS, 2 * HD]), ALU.mult)\
                  .then_inc(S["rms_ready"], 1)

            def second_norm(g):
                step(add(of_group(xin, g), of_group(xin, g), row("n2_b", TG)))
                dve.wait_ge(S["wo_done"], g + 1)
                moments(1, g, tiled(bank(2 + g)))
                shifted_variance(1, 2, g)

            def residual(g):
                dve.wait_ge(s_rstd[2], g + 1)
                src = tiled(bank(2 + g))
                w = row_sb[:, ROW["n2_w"][0]:ROW["n2_w"][0] + P]
                for t in range(TG):
                    step(nc.vector.scalar_tensor_tensor(of_group(tmp, g)[:, t], src[:, t], mv[:, 1, g, t, 0:1], w,
                                                        ALU.subtract, ALU.mult))
                settle()
                for t in range(TG):
                    ins = nc.vector.scalar_tensor_tensor(of_group(h, g)[:, t], of_group(tmp, g)[:, t],
                                                         rstd[:, 2, g, t:t + 1], of_group(xin, g)[:, t],
                                                         ALU.mult, ALU.add)
                ins.then_inc(S["h_ready"], 1)
                dve.wait_ge(S["h_ready"], g + 1)
                moments(2, g, of_group(h, g))
                shifted_variance(2, 3, g)
                step(add(of_group(hsum, g), of_group(h0, g), of_group(h, g)))
                settle()
                step(add(of_group(hsum, g), of_group(hsum, g), row("mb2", TG)))

            def third_norm(g):
                dve.wait_ge(s_rstd[3], g + 1)
                normalise(of_group(cent, g), of_group(h, g), 2, 3, g).then_inc(S["zc_ready"], 1)

            def mlp_bias(g):
                for t in range(g * TG, (g + 1) * TG):
                    dve.wait_ge(S["w1_done"], t + 1)
                    add(hid[:, t], bank(6 + t % 2), row_sb[:, ROW["mb1"][0]:ROW["mb1"][0] + HID])\
                        .then_inc(S["w1_read"], 1)

            def hidden_moments(g):
                for t in range(TG):
                    dve.wait_ge(S["gelu_ready"], g * TG + t + 1)
                    step(nc.vector.bn_stats(stats[:, t], hid[:, g * TG + t]))
                settle()
                for t in range(TG):
                    step(nc.vector.bn_aggr(mv[:, 3, g, t], stats[:, t]))
                settle()
                shifted_variance(3, 4, g)

            def hidden_norm(g):
                dve.wait_ge(s_rstd[4], g + 1)
                normalise(of_group(hid, g), of_group(hid, g), 3, 4, g).then_inc(S["hidn_ready"], 1)

            def mlp_out(g):
                settle()
                dve.wait_ge(S["w2_done"], g + 1)
                add(of_group(h1, g), tiled(bank(4 + g)), of_group(hsum, g)).then_inc(S["h1_ready"], 1)
                dve.wait_ge(S["h1_ready"], g + 1)
                moments(4, g, of_group(h1, g))
                double_variance(4, 5, g)

            def ffn_norm(g):
                dve.wait_ge(s_rstd[5], g + 1)
                normalise(of_group(cent, g), of_group(h1, g), 4, 5, g, second=1)
                normalise(of_group(xin, g), of_group(h1, g), 4, 5, g).then_inc(S["n_ready"], 1)

            def expert_out(g):
                dve.wait_ge(S["fc2_done"], (g + 1) * TG)
                at = COL["fc2_b"][0] + g * TG
                add(tiled(kT[:, g]), tiled(bank(4 + g)), col_sb[:, at:at + TG][:, :, None].to_broadcast([P, TG, P]))\
                    .then_inc(S["yT_ready"], 1)

            def next_bias(g):
                dve.wait_ge(S["next_done"], g + 1)
                add(of_group(tmp, g), tiled(bank(6 + g)), row("next_b", TG)).then_inc(S["next_read"], 1)

            def output(g):
                dve.wait_ge(S["ngelu_ready"], g + 1)
                add(of_group(tmp, g), of_group(tmp, g), of_group(h1, g)).then_inc(S["out_ready"], 1)

            embedding(0)
            input_norm(0)
            embedding(1)
            values(0)
            input_norm(1)
            values(1)
            softmax_shift(0)
            for t in range(TILES):
                if t + 1 < TILES:
                    softmax_shift(t + 1)
                if t >= 1:
                    difference(t - 1)
            difference(TILES - 1)
            for stage in (rms, rms_apply, second_norm, residual, third_norm, mlp_bias, hidden_moments, hidden_norm,
                          mlp_out, ffn_norm, expert_out, next_bias, output):
                for g in range(G):
                    stage(g)

        @block.tensor
        def _(pe):
            mm = nc.tensor.matmul

            def turn(dst, src):
                return nc.tensor.transpose(dst, src, ident[:])

            def tokens(g):
                if g == 0:
                    pe.wait_ge(s_tokw, 16)
                for c in range(KC):
                    pe.wait_ge(s_x[g][c], 16)
                    for t in range(TG):
                        ins = mm(bank(g)[:, t * P:(t + 1) * P], x_sb[:, g, c, t * P:(t + 1) * P], tokw[:, c],
                                 start=(c == 0 and t == 0), stop=(c == KC - 1), skip_group_check=True)
                ins.then_inc(S["tok_done"], 1)

            def turn_group(dst, src, g):
                for t in range(TG):
                    ins = turn(dst[:, t * P:(t + 1) * P], src[:, g * TG + t])
                return ins

            def input_norm(g):
                if g == 0:
                    pe.wait_ge(s_ident, 1)
                pe.wait_ge(S["xc_ready"], g + 1)
                turn_group(bank(2 + g), cent, g).then_inc(S["xcT_done"], 1)

            def projections(g):
                if g == 0:
                    pe.wait_ge(s_qkvo, 16)
                pe.wait_ge(S["xnT_ready"], g + 1)
                if g > 0:
                    pe.wait_ge(S["kT_ready"], g)
                mm(bank(5), qkvo[:, 1], xnT[:, g], start=True, stop=True).then_inc(S["k_done"], 1)
                if g > 0:
                    pe.wait_ge(S["qT_ready"], g)
                mm(bank(4), qkvo[:, 0], xnT[:, g], start=True, stop=True).then_inc(S["q_done"], 1)
                if g > 0:
                    pe.wait_ge(S["vdiag_ready"], 2 * g)
                for i in range(2):
                    for b in range(4):
                        at = (4 * i + b) * N
                        for j in range(2):
                            ins = mm(bank(6 + i)[j * N:(j + 1) * N, b * P:(b + 1) * P], xnT[:, g, at:at + N],
                                     qkvo[:, 2], start=True, stop=True)
                    ins.then_inc(S["v_done"], 1)

            def scores(t):
                g = t // TG
                if t < 2:
                    pe.wait_ge(S["h0_ready"] if t == 0 else S["xnT_ready"], G)
                else:
                    pe.wait_ge(S["shifted"], t - 1)
                pe.wait_ge(S["qT_ready"], g + 1)
                pe.wait_ge(s_kdiag[g], 16 * SUB)
                for r, b in ((0, 0), (1, 1), (0, 1), (1, 0)):
                    rows_r = slice(64 * r, 64 * r + 64)
                    at = ((t % TG) * NB + b) * N
                    ins = mm(pairs[t % 2][b * N:(b + 1) * N, r * COLS:(r + 1) * COLS], qT[rows_r, g, at:at + N],
                             kdiag[rows_r, t * NB + b].rearrange("p s n -> p (s n)"), start=True, stop=True)
                ins.then_inc(S["s_done"], 1)

            def turn_probs(t):
                pe.wait_ge(S["exp_done"], t + 1)
                if t == 0:
                    pe.wait_ge(S["qT_ready"], G)
                    pe.wait_ge(S["kT_ready"], G)
                else:
                    pe.wait_ge(S["probT_ready"], t)
                for hd in range(HEADS):
                    ins = turn(pairs[2][:, hd * P:(hd + 1) * P],
                               prob[:, t % 2, 2 * hd:2 * hd + 2].rearrange("p s n -> p (s n)"))
                ins.then_inc(S["probT_done"], 1)

            def attend(t):
                pe.wait_ge(S["probT_ready"], t + 1)
                pe.wait_ge(S["vdiag_ready"], 2 * G if t == 0 else 2 * (t // TG + 1))
                if t == 0:
                    pe.wait_ge(s_ones, 2)
                else:
                    pe.wait_ge(S["o_read"], t)
                for hd in range(HEADS):
                    ins = mm(pairs[3][:, hd * OH:hd * OH + 2 * NB * VC], probT[:, t % 2, hd],
                             vdiag[:, t * NB:(t + 1) * NB, hd].rearrange("p b j c -> p b (j c)"),
                             start=True, stop=True)
                ins.then_inc(S["o_done"], 1)

            def attention_out(g):
                pe.wait_ge(S["rms_ready"], g + 1)
                pe.wait_ge(S["shifted"], TILES)
                turn_group(bank(g), cent, g).then_inc(S["aT_done"], 1)
                pe.wait_ge(S["aT_ready"], g + 1)
                for t in range(TG):
                    ins = mm(bank(2 + g)[:, t * P:(t + 1) * P], xnT[:, g, t * P:(t + 1) * P], qkvo[:, 3],
                             start=True, stop=True)
                ins.then_inc(S["wo_done"], 1)

            def mlp_up(g):
                pe.wait_ge(S["zc_ready"], g + 1)
                pe.wait_ge(S["probT_ready"], TILES)
                turn_group(bank(4 + g), cent, g).then_inc(S["zcT_done"], 1)
                if g == 0:
                    pe.wait_ge(s_w1, 16)
                pe.wait_ge(S["zT_ready"], g + 1)
                for t in range(TG):
                    n = g * TG + t
                    if n < 2:
                        pe.wait_ge(S["o_read"], TILES)
                    else:
                        pe.wait_ge(S["w1_read"], n - 1)
                    mm(bank(6 + n % 2), qT[:, g, t * P:(t + 1) * P], w1[:], start=True, stop=True)\
                        .then_inc(S["w1_done"], 1)

            def turn_hidden(g):
                pe.wait_ge(S["hidn_ready"], g + 1)
                for c in range(HC):
                    if g == 0:
                        pe.wait_ge(S["h_ready"], G)
                    else:
                        pe.wait_ge(S["hidT_ready"], (g - 1) * HC + c + 1)
                    for t in range(TG):
                        ins = turn(bank(c)[:, t * P:(t + 1) * P], hid[:, g * TG + t, c * P:(c + 1) * P])
                    ins.then_inc(S["hidT_done"], 1)

            def mlp_down(g):
                if g == 0:
                    pe.wait_ge(s_w2, 16)
                pe.wait_ge(S["hidT_ready"], (g + 1) * HC)
                for t in range(TG):
                    for c in range(HC):
                        ins = mm(bank(4 + g)[:, t * P:(t + 1) * P], hidT[:, c, t * P:(t + 1) * P], w2[:, c],
                                 start=(c == 0), stop=(c == HC - 1))
                ins.then_inc(S["w2_done"], 1)

            def ffn_in(g):
                if g == 0:
                    pe.wait_ge(s_wan, 32)
                    pe.wait_ge(S["w1_read"], TILES)
                else:
                    pe.wait_ge(S["nT_ready"], g)
                pe.wait_ge(S["n_ready"], g + 1)
                turn_group(bank(6), cent, g).then_inc(S["nT_done"], 1)
                pe.wait_ge(S["nT_ready"], g + 1)
                if g > 0:
                    pe.wait_ge(S["xaT_ready"], g)
                mm(bank(7), wattn[:], xnT[:, g], start=True, stop=False, skip_group_check=True)
                for t in range(TG):
                    ins = mm(bank(7)[:, t * P:(t + 1) * P], xin[:, g * TG + t], ident[:], start=False,
                             stop=(t == TG - 1), skip_group_check=True)
                ins.then_inc(S["xa_done"], 1)

            def expert_up(e):
                g, t = e // TG, e % TG
                pe.wait_ge(s_fc1[e], 16)
                pe.wait_ge(S["xaT_ready"], g + 1)
                if e < 4:
                    pe.wait_ge(S["hidT_ready"], G * HC)
                else:
                    pe.wait_ge(S["fgelu_ready"], e - 3)
                for c in range(HC):
                    ins = mm(bank(e % 4)[:, c * P:(c + 1) * P], fc1[:, e, c * P:(c + 1) * P],
                             qT[:, g, t * P:(t + 1) * P], start=True, stop=True)
                ins.then_inc(S["fc1_done"], 1)

            def expert_down(e):
                g, t = e // TG, e % TG
                pe.wait_ge(s_fc2[e], 16)
                pe.wait_ge(S["fgelu_ready"], e + 1)
                if e == 0:
                    pe.wait_ge(S["h1_ready"], G)
                for c in range(HC):
                    ins = mm(bank(4 + g)[:, t * P:(t + 1) * P], fc2[:, e, c], hid[:, e, c * P:(c + 1) * P],
                             start=(c == 0), stop=(c == HC - 1))
                ins.then_inc(S["fc2_done"], 1)

            def next_layer(g):
                pe.wait_ge(S["yT_ready"], g + 1)
                pe.wait_ge(S["xaT_ready"], G)
                for t in range(TG):
                    ins = mm(bank(6 + g)[:, t * P:(t + 1) * P], kT[:, g, t * P:(t + 1) * P], wnext[:],
                             start=True, stop=True)
                ins.then_inc(S["next_done"], 1)

            tokens(0)
            input_norm(0)
            tokens(1)
            projections(0)
            input_norm(1)
            projections(1)
            scores(0)
            for t in range(TILES):
                if t + 1 < TILES:
                    scores(t + 1)
                turn_probs(t)
                if t >= 1:
                    attend(t - 1)
            attend(TILES - 1)
            for stage in (attention_out, mlp_up, turn_hidden, mlp_down, ffn_in):
                for g in range(G):
                    stage(g)
            expert_up(0)
            for e in range(TILES):
                if e + 1 < TILES:
                    expert_up(e + 1)
                expert_down(e)
            for g in range(G):
                next_layer(g)


def kernel(x, L0_tok_w, L0_tok_b, L0_attn_Wq, L0_attn_Wk, L0_attn_Wv, L0_attn_Wo, L0_attn_lq1, L0_attn_lk1,
           L0_attn_lq2, L0_attn_lk2, L0_attn_subln_w, L0_attn_n1_w, L0_attn_n1_b, L0_attn_n2_w, L0_attn_n2_b,
           L0_attn_mln1_w, L0_attn_mln1_b, L0_attn_mW1, L0_attn_mb1, L0_attn_mln2_w, L0_attn_mln2_b, L0_attn_mW2,
           L0_attn_mb2, L0_ffn_ln_g, L0_ffn_ln_b, L0_ffn_attn_w, L0_ffn_attn_b, L0_ffn_gate_w, L0_ffn_fc1_w,
           L0_ffn_fc1_b, L0_ffn_fc2_w, L0_ffn_fc2_b, L0_ffn_next_w, L0_ffn_next_b):
    import numpy as np
    import concourse.bacc as bacc
    from concourse.bass_utils import run_bass_kernel_spmd

    def vectors(a):
        return np.asarray(a).reshape(-1, P).T

    side = np.asarray(x).shape[2] // 16
    px = np.asarray(x).reshape(NB, G, TG, 3, side, 16, side, 16).transpose(3, 5, 7, 1, 2, 0, 4, 6)
    px = px.reshape(KC, P, G, COLS).transpose(2, 0, 1, 3)
    columns = {"n1_w": L0_attn_n1_w, "n1_b": L0_attn_n1_b, "subln_w": np.tile(np.asarray(L0_attn_subln_w), HEADS),
               "mln1_w": L0_attn_mln1_w, "mln1_b": L0_attn_mln1_b, "mln2_w": L0_attn_mln2_w,
               "mln2_b": L0_attn_mln2_b, "ln_g": L0_ffn_ln_g, "ln_b": L0_ffn_ln_b, "attn_b": L0_ffn_attn_b,
               "fc1_b": L0_ffn_fc1_b, "fc2_b": L0_ffn_fc2_b}
    lam = np.concatenate([np.asarray(v) for v in (L0_attn_lq1, L0_attn_lk1, L0_attn_lq2, L0_attn_lk2)])
    rows = {"tok_b": L0_tok_b, "n2_w": L0_attn_n2_w, "n2_b": L0_attn_n2_b, "mb2": L0_attn_mb2,
            "next_b": L0_ffn_next_b, "mb1": L0_attn_mb1, "lam": lam}
    arrays = {
        "xT": px,
        "tok_wT": np.asarray(L0_tok_w).T.reshape(KC, P, P),
        "cols": np.concatenate([vectors(columns[n]) for n in COL], axis=1),
        "rows": np.concatenate([np.asarray(rows[n]).reshape(1, -1) for n in ROW], axis=1),
        "qkvoT": np.stack([np.asarray(w).T for w in (L0_attn_Wq, L0_attn_Wk, L0_attn_Wv, L0_attn_Wo)], axis=1),
        "w1T": np.asarray(L0_attn_mW1).T,
        "w2T": np.asarray(L0_attn_mW2).T.reshape(HC, P, P),
        "attnT": np.asarray(L0_ffn_attn_w).T,
        "nextT": np.asarray(L0_ffn_next_w).T,
        "fc1T": np.asarray(L0_ffn_fc1_w).transpose(0, 2, 1),
        "fc2T": np.asarray(L0_ffn_fc2_w).transpose(0, 2, 1).reshape(TILES, HC, P, P).transpose(0, 2, 1, 3),
    }
    arrays = {k: np.ascontiguousarray(v) for k, v in arrays.items()}
    nc = bacc.Bacc("TRN2", target_bir_lowering=False, num_devices=1)
    args = [nc.dram_tensor(n, a.shape, mybir.dt.from_np(a.dtype), kind="ExternalInput").ap() for n, a in arrays.items()]
    out = nc.dram_tensor("out", (G, P, TG, P), mybir.dt.float32, kind="ExternalOutput").ap()
    vit_layer(nc, *args, out)
    r = run_bass_kernel_spmd(nc, [arrays], core_ids=[0])
    y = r.results[0]["out"].reshape(G, NB, N, TG, P).transpose(1, 0, 3, 2, 4)
    return np.ascontiguousarray(y.reshape(NB * G * TG, N, P))
```

```python
import concourse.bass as bass
from concourse import mybir
from contextlib import ExitStack

P = 128
TILES = 8
G = 4
TG = TILES // G
COLS = TG * P
KC = 6
HEADS = 8
HD = 8
NB = 2
N = 64
SUB = 2 * HEADS
VC = 2 * HD + 1
OH = 128
HC = 4
HID = HC * P
EPS = 1e-5
LAMBDA_INIT = 0.8 - 0.6 * 1.0

COL = {}
for _name, _n in (("n1_w", 1), ("n1_b", 1), ("subln_w", 1), ("mln1_w", 1), ("mln1_b", 1), ("mln2_w", HC),
                  ("mln2_b", HC), ("ln_g", 1), ("ln_b", 1), ("attn_b", 1), ("fc1_b", TILES * HC),
                  ("fc2_b", TILES)):
    COL[_name] = sum(n for _, n in COL.values()), _n
NCOL = sum(n for _, n in COL.values())
ROW = {}
for _name, _n in (("tok_b", P), ("n2_w", P), ("n2_b", P), ("mb2", P), ("next_b", P), ("mb1", HID), ("lam", 4 * HD)):
    ROW[_name] = sum(n for _, n in ROW.values()), _n
NROW = sum(n for _, n in ROW.values())


START = {
    "constants": [-1],
    "lam_dots": [0.0],
    "lam_exps": [-1.9],
    "lam": [7.8],
    "fold_weights": [15.1],
    "fold_sums": [16],
    "fold_rows": [17],
    "tokens": [2.5, 6.8, 7.6, 17.9],
    "embedding": [3.9, 8.2, 9, 19.3],
    "root0": [4.9, 10.5, 11.2, 20.3],
    "input_norm": [8.7, 11.0, 11.9, 23.1],
    "turn_input": [7.9, 12.2, 13, 22.9],
    "input_affine": [5.9, 12.7, 13.5, 23.8],
    "project_qk": [9.5, 13.8, 14, 24.3],
    "qk_out": [10.2, 14.5, 15.3, 25.5],
    "spread_k": [5.4, 14.7, 15.5, 27.3],
    "project_v": [10.2, 14.5, 15.2, 23.7],
    "values": [11.4, 14.7, 16.5, 26.8],
    "scores": [16.0, 21.6, 26.9, 32.9, 38.0, 39.1, 47.2, 56.0],
    "softmax_shift": [18.6, 24.2, 28.7, 35.5, 40.6, 41.7, 49.8, 58.6],
    "exponentials": [20.5, 26.1, 31.4, 37.4, 42.5, 43.1, 51.7, 60.5],
    "turn_probs": [22.0, 27.6, 32.9, 38.9, 44.0, 45.1, 53.7, 62.0],
    "probs_out": [22.4, 28.6, 33.2, 39.9, 45.0, 46.1, 54.2, 63.0],
    "attend": [25.3, 30.8, 36.2, 42.2, 45.6, 48.3, 56.4, 65.2],
    "difference": [26.5, 32.1, 37.4, 43.4, 48.5, 49.6, 57.7, 66.5],
    "rms": [34.5, 45.5, 55.1, 67.8],
    "root1": [37, 48, 57.6, 68.9],
    "rms_apply": [39.7, 51, 60.6, 73.2],
    "turn_attn": [41, 52, 60.6, 73.5],
    "attn_affine": [42.4, 52.8, 61.8, 74.4],
    "attn_out": [44.4, 53.5, 62.5, 75.1],
    "second_moments": [42.6, 54.5, 63.5, 76.1],
    "root2": [44.5, 55.9, 64.5, 77.1],
    "residual": [45.0, 56.1, 65.5, 78.1],
    "root3": [47.6, 58.9, 67.5, 79.3],
    "mlp_norm": [49.3, 59.9, 68.5, 81.1],
    "turn_mlp": [49.0, 59.2, 69.5, 82.1],
    "mlp_affine": [49.5, 60.9, 69.5, 82.1],
    "mlp_up": [51, 52, 62.4, 63.4, 71.0, 71.1, 83.6, 84.6],
    "mlp_bias": [52, 53, 63.4, 64.4, 72.0, 73.0, 84.6, 85.6],
    "mlp_gelu": [53, 54, 64.4, 65.4, 73.0, 74.0, 85.6, 86.6],
    "sums": [45.4, 58.4, 67.0, 79.6],
    "turn_hidden": [55.2, 66.3, 75.0, 87.6],
    "hidden_out": [56.2, 67.4, 76.0, 88.6],
    "hidden_moments": [55.7, 66.9, 75.5, 87.8],
    "root4": [56.2, 67.4, 76.0, 88.6],
    "mlp_down": [56.5, 68.4, 77.0, 89.6],
    "mlp_result": [59.2, 70.4, 79.0, 91.0],
    "root5": [62.2, 73.4, 83.4, 94.8],
    "ffn_norm": [61.2, 72.4, 81.5, 93.5],
    "turn_ffn": [62.2, 73.4, 83.4, 94.0],
    "ffn_affine": [62.7, 73.7, 83.7, 92.9],
    "ffn_tokens": [63.7, 74.9, 84.7, 99.1],
    "ffn_tokens_out": [63.8, 74.6, 87.5, 99.4],
    "expert_up": [65.7, 66.7, 76.9, 77.9, 90.0, 92.0, 101.3, 102.3],
    "expert_gelu": [66.7, 67.7, 77.9, 78.9, 91.0, 92.0, 104.7, 107.6],
    "expert_down": [68.5, 69.5, 78.9, 79.9, 92.0, 92.3, 105.7, 106.7],
    "expert_out": [71.0, 79.8, 94.5, 108.2],
    "next_layer": [71.5, 87.7, 97.0, 121.3],
    "next_bias": [72.0, 88.5, 97.5, 112.1],
    "last_gelu": [72.5, 89.0, 98.0, 110.5],
    "output": [73.6, 90.0, 99.0, 113.9],
    "store": [78.2, 87.4, 96.9, 109.4],
}


def in_order(stages):
    turns = [(at, i, stage, n) for i, stage in enumerate(stages) for n, at in enumerate(START[stage.__name__])]
    for _, _, stage, n in sorted(turns, key=lambda x: x[:2] + x[3:]):
        yield stage, n


def vit_layer(nc, xT, tok_wT, cols, rows, qkvoT, w1T, w2T, attnT, nextT, fc1T, fc2T, out):
    fp32 = mybir.dt.float32
    ALU = mybir.AluOpType
    ACT = mybir.ActivationFunctionType
    AX = mybir.AxisListType.X

    ctx = ExitStack()
    with ctx:
        def sb(name, shape):
            return ctx.enter_context(nc.sbuf_tensor(name, shape, fp32))

        def sem(name):
            return ctx.enter_context(nc.semaphore(name))

        x_sb = sb("x_sb", [P, G, KC, COLS])
        tokw = sb("tokw", [P, KC, P])
        col_sb = sb("col_sb", [P, NCOL])
        row_sb = sb("row_sb", [P, NROW])
        qkvo = sb("qkvo", [P, 4, P])
        w1 = sb("w1", [P, HID])
        w2 = sb("w2", [P, HC, P])
        w2n = sb("w2n", [P, HC, P])
        wattn = sb("wattn", [P, P])
        wnext = sb("wnext", [P, P])
        fc1 = sb("fc1", [P, TILES, HID])
        fc2 = sb("fc2", [P, TILES, HC, P])
        ident = sb("ident", [P, P])
        ones = sb("ones", [P, P])
        mln2_b = sb("mln2_b", [P, HC, P])
        w2n_sums = sb("w2n_sums", [P, P])
        mlp_row = sb("mlp_row", [P, P])
        exponent = sb("exponent", [P, TG * HEADS])
        sub_scale = sb("sub_scale", [P, 1])
        lam_prod = sb("lam_prod", [P, 2, HD])
        lam_dot = sb("lam_dot", [P, 2])
        lam_exp = sb("lam_exp", [P, 2])
        lam_diff = sb("lam_diff", [P, 1])
        neg_lam = sb("neg_lam", [P, 1])
        h0 = sb("h0", [P, TILES, P])
        xin = sb("xin", [P, TILES, P])
        cent = sb("cent", [P, TILES, P])
        attn = sb("attn", [P, TILES, HEADS, 2 * HD])
        h = sb("h", [P, TILES, P])
        hsum = sb("hsum", [P, TILES, P])
        h1 = sb("h1", [P, TILES, P])
        hid = sb("hid", [P, TILES, HID])
        xnT = sb("xnT", [P, G, COLS])
        qT = sb("qT", [P, G, COLS])
        kT = sb("kT", [P, G, COLS])
        hidT = x_sb[:, :, 0:HC]
        kdiag = sb("kdiag", [P, TILES * NB, SUB // 2, N])
        vdiag = sb("vdiag", [P, TILES * NB, HEADS, 2, VC])
        prob = sb("prob", [P, 2, SUB, N])
        probT = sb("probT", [P, 2, HEADS, P])
        negmax = sb("negmax", [P, 2, SUB])
        rden = sb("rden", [P, 2, HEADS, 2])
        onorm = sb("onorm", [P, 2, HEADS, 2, 2 * HD])
        stats = sb("stats", [P, 5, TG, 6])
        mv = sb("mv", [P, 5, G, TG, 2])
        var = sb("var", [P, 6, G, TG * HEADS])
        rstd = sb("rstd", [P, 6, G, TG * HEADS])
        nmr = sb("nmr", [P, G, TG])

        score_ps = ctx.enter_context(nc.psum_tensor("score_ps", [P, SUB, N], fp32))
        turned_ps = ctx.enter_context(nc.psum_tensor("turned_ps", [P, HEADS, P], fp32))
        value_ps = ctx.enter_context(nc.psum_tensor("value_ps", [P, HEADS, 2, VC], fp32))
        ring = [ctx.enter_context(nc.psum_tensor(f"ring{i}", [P, HID], fp32)) for i in range(3)]

        def col(name, i=0):
            at = COL[name][0] + i
            return col_sb[:, at:at + 1]

        def row(name):
            at, n = ROW[name]
            return row_sb[:, at:at + n]

        def over_tiles(ap):
            return ap[:, None, :].to_broadcast([P, TG, ap.shape[1]])

        def tiled(ap):
            return ap[:, 0:COLS].rearrange("p (t n) -> p t n", n=P)

        def of_group(t, g):
            return t[:, g * TG:(g + 1) * TG]

        def scratch(g):
            return tiled(x_sb[:, g, HC])

        s_tokw, s_col, s_row, s_qkvo = sem("tokw_in"), sem("cols_in"), sem("rows_in"), sem("qkvo_in")
        XH = 2
        s_x = [[sem(f"x_in_{g}_{i}") for i in range(XH)] for g in range(G)]
        s_w1, s_w2, s_wan = sem("w1_in"), sem("w2_in"), sem("wattn_wnext_in")
        s_fc = [sem(f"fc_in_{e}") for e in range(TILES)]
        s_kdiag = [sem(f"kdiag_ready_{g}") for g in range(G)]
        s_ident0, s_ident, s_half, s_zero = (sem("ident_cleared"), sem("ident_ready"), sem("exponent_ready"),
                                             sem("diags_cleared"))
        s_ones = sem("ones_ready")
        s_lamdot, s_lamexp, s_subs = sem("lam_dots"), sem("lam_exps"), sem("sub_scale_ready")
        s_w2n, s_w2sums, s_w2rows = sem("w2n_ready"), sem("w2n_sums_done"), sem("mlp_rows_ready")
        s_dve = sem("vector_steps")
        s_var = [sem(f"var_ready_{k}") for k in range(6)]
        s_rstd = [sem(f"rstd_ready_{k}") for k in range(6)]
        names = ("tok_done h0_ready xin_ready xc_ready xcT_done xnT_ready qk_done kT_ready qT_ready "
                 "v_done vdiag_ready s_done shifted exp_done probT_done probT_ready o_done o_read rms_ready aT_done "
                 "aT_ready wo_done h_ready hsum_ready zc_ready zcT_done zT_ready w1_done w1_read gelu_ready "
                 "hidT_done hidT_ready w2_done h1_ready n_ready nT_done nT_ready xa_done xaT_ready fc1_done "
                 "fgelu_ready fc2_done yT_ready next_done next_read ngelu_ready out_ready stored").split()
        S = {n: sem(n) for n in names}

        block = ctx.enter_context(nc.Block())

        RING_USES = {"tokens": "h0_ready", "turn_input": "xnT_ready", "project_qk": "qT_ready",
                     "project_v": "vdiag_ready", "turn_attn": "aT_ready", "attn_out": "h_ready",
                     "turn_mlp": "zT_ready", "mlp_up": "w1_read", "turn_hidden": "hidT_ready",
                     "mlp_down": "h1_ready", "turn_ffn": "nT_ready", "ffn_tokens": "xaT_ready",
                     "expert_up": "fgelu_ready", "expert_down": "yT_ready", "next_layer": "next_read",
                     "fold_sums": "mlp_rows_ready"}
        bank_of, readers_before = {}, {}

        def deal_banks(stages):
            last, turn = [None] * len(ring), 0
            for stage, n in in_order(stages):
                name = stage.__name__
                if name not in RING_USES or (name == "expert_down" and n % TG):
                    continue
                reader = s_w2rows if name == "fold_sums" else S[RING_USES[name]]
                for i in range(2 if name == "turn_hidden" else 1):
                    b = turn % len(ring)
                    count = 2 * n + i + 1 if name == "turn_hidden" else n // TG + 1 if name == "expert_down" else n + 1
                    bank_of[name, n, i], readers_before[name, n, i] = ring[b], last[b]
                    last[b] = reader, count
                    turn += 1

        def pe_stages():
            mm = nc.tensor.matmul
            pe = nc.tensor

            def turn(dst, src):
                return nc.tensor.transpose(dst, src, ident[:])

            def take(name, n, i=0):
                if readers_before[name, n, i]:
                    pe.wait_ge(*readers_before[name, n, i])
                return bank_of[name, n, i]

            def turn_group(name, src, g):
                dst = take(name, g)
                for t in range(TG):
                    ins = turn(dst[:, t * P:(t + 1) * P], src[:, g * TG + t])
                return ins

            def tokens(g):
                if g == 0:
                    pe.wait_ge(s_tokw, 16)
                dst = take("tokens", g)
                for c in range(KC):
                    if c % (KC // XH) == 0:
                        pe.wait_ge(s_x[g][c // (KC // XH)], 16)
                    for t in range(TG):
                        ins = mm(dst[:, t * P:(t + 1) * P], x_sb[:, g, c, t * P:(t + 1) * P], tokw[:, c],
                                 start=(c == 0 and t == 0), stop=(c == KC - 1), skip_group_check=True)
                ins.then_inc(S["tok_done"], 1)

            def turn_input(g):
                if g == 0:
                    pe.wait_ge(s_ident, 1)
                pe.wait_ge(S["xc_ready"], g + 1)
                turn_group("turn_input", cent, g).then_inc(S["xcT_done"], 1)

            def project_qk(g):
                if g == 0:
                    pe.wait_ge(s_qkvo, 16)
                pe.wait_ge(S["xnT_ready"], g + 1)
                dst = take("project_qk", g)
                mm(dst[:, COLS:2 * COLS], qkvo[:, 1], xnT[:, g], start=True, stop=True)
                mm(dst[:, 0:COLS], qkvo[:, 0], xnT[:, g], start=True, stop=True).then_inc(S["qk_done"], 1)

            def project_v(g):
                pe.wait_ge(S["xnT_ready"], g + 1)
                dst = take("project_v", g)
                for b in range(TG * NB):
                    for j in range(2):
                        ins = mm(dst[j * N:(j + 1) * N, b * P:(b + 1) * P], xnT[:, g, b * N:(b + 1) * N],
                                 qkvo[:, 2], start=True, stop=True)
                ins.then_inc(S["v_done"], 1)

            def scores(t):
                g = t // TG
                if t > 0:
                    pe.wait_ge(S["shifted"], t)
                pe.wait_ge(S["qT_ready"], g + 1)
                pe.wait_ge(s_kdiag[g], 16 * SUB // 2)
                for r, b in ((0, 0), (1, 1), (0, 1), (1, 0)):
                    rows_r = slice(64 * r, 64 * r + 64)
                    at = ((t % TG) * NB + b) * N
                    ins = mm(score_ps[b * N:(b + 1) * N, r * SUB // 2:(r + 1) * SUB // 2], qT[rows_r, g, at:at + N],
                             kdiag[rows_r, t * NB + b], start=True, stop=True)
                ins.then_inc(S["s_done"], 1)

            def turn_probs(t):
                pe.wait_ge(S["exp_done"], t + 1)
                if t > 0:
                    pe.wait_ge(S["probT_ready"], t)
                for hd in range(HEADS):
                    ins = turn(turned_ps[:, hd], prob[:, t % 2, 2 * hd:2 * hd + 2].rearrange("p s n -> p (s n)"))
                ins.then_inc(S["probT_done"], 1)

            def attend(t):
                pe.wait_ge(S["probT_ready"], t + 1)
                pe.wait_ge(S["vdiag_ready"], t // TG + 1)
                if t == 0:
                    pe.wait_ge(s_ones, 3)
                else:
                    pe.wait_ge(S["o_read"], t)
                for hd in range(HEADS):
                    for b in range(NB):
                        ins = mm(value_ps[b * N:(b + 1) * N, hd], probT[:, t % 2, hd, b * N:(b + 1) * N],
                                 vdiag[:, t * NB + b, hd], start=True, stop=True)
                ins.then_inc(S["o_done"], 1)

            def turn_attn(g):
                pe.wait_ge(S["rms_ready"], g + 1)
                turn_group("turn_attn", cent, g).then_inc(S["aT_done"], 1)

            def attn_out(g):
                pe.wait_ge(S["aT_ready"], g + 1)
                dst = take("attn_out", g)
                for t in range(TG):
                    ins = mm(dst[:, t * P:(t + 1) * P], xnT[:, g, t * P:(t + 1) * P], qkvo[:, 3],
                             start=True, stop=True)
                ins.then_inc(S["wo_done"], 1)

            def turn_mlp(g):
                pe.wait_ge(S["zc_ready"], g + 1)
                turn_group("turn_mlp", cent, g).then_inc(S["zcT_done"], 1)

            def mlp_up(t):
                if t == 0:
                    pe.wait_ge(s_w1, 16)
                pe.wait_ge(S["zT_ready"], t // TG + 1)
                at = (t % TG) * P
                mm(take("mlp_up", t)[:], qT[:, t // TG, at:at + P], w1[:], start=True, stop=True)\
                    .then_inc(S["w1_done"], 1)

            def fold_sums(n):
                pe.wait_ge(s_w2n, 1)
                pe.wait_ge(s_ones, 3)
                dst = take("fold_sums", 0)
                for c in range(HC):
                    mm(dst[:, 0:P], ones[:], w2n[:, c], start=(c == 0), stop=(c == HC - 1))
                for c in range(HC):
                    ins = mm(dst[:, P:2 * P], mln2_b[:, c], w2[:, c], start=(c == 0), stop=(c == HC - 1))
                ins.then_inc(s_w2sums, 1)

            def turn_hidden(g):
                for i in range(2):
                    dst = take("turn_hidden", g, i)
                    for c in range(2):
                        for t in range(TG):
                            pe.wait_ge(S["gelu_ready"], g * TG + t + 1)
                            at = (2 * i + c) * P
                            ins = turn(dst[:, c * COLS + t * P:c * COLS + (t + 1) * P],
                                       hid[:, g * TG + t, at:at + P])
                    ins.then_inc(S["hidT_done"], 1)

            def mlp_down(g):
                if g == 0:
                    pe.wait_ge(s_w2n, 1)
                pe.wait_ge(S["hidT_ready"], 2 * (g + 1))
                dst = take("mlp_down", g)
                for t in range(TG):
                    for c in range(HC):
                        ins = mm(dst[:, t * P:(t + 1) * P], hidT[:, g, c, t * P:(t + 1) * P], w2n[:, c],
                                 start=(c == 0), stop=(c == HC - 1))
                ins.then_inc(S["w2_done"], 1)

            def turn_ffn(g):
                pe.wait_ge(S["n_ready"], g + 1)
                turn_group("turn_ffn", cent, g).then_inc(S["nT_done"], 1)

            def ffn_tokens(g):
                if g == 0:
                    pe.wait_ge(s_wan, 32)
                pe.wait_ge(S["nT_ready"], g + 1)
                dst = take("ffn_tokens", g)
                mm(dst[:, 0:COLS], wattn[:], xnT[:, g], start=True, stop=False, skip_group_check=True)
                for t in range(TG):
                    ins = mm(dst[:, t * P:(t + 1) * P], xin[:, g * TG + t], ident[:], start=False,
                             stop=(t == TG - 1), skip_group_check=True)
                ins.then_inc(S["xa_done"], 1)

            def expert_up(e):
                g, t = e // TG, e % TG
                pe.wait_ge(s_fc[e], 32)
                pe.wait_ge(S["xaT_ready"], g + 1)
                dst = take("expert_up", e)
                for c in range(HC):
                    ins = mm(dst[:, c * P:(c + 1) * P], fc1[:, e, c * P:(c + 1) * P],
                             qT[:, g, t * P:(t + 1) * P], start=True, stop=True)
                ins.then_inc(S["fc1_done"], 1)

            def expert_down(e):
                t = e % TG
                pe.wait_ge(S["fgelu_ready"], e + 1)
                dst = take("expert_down", e) if t == 0 else bank_of["expert_down", e - t, 0]
                for c in range(HC):
                    ins = mm(dst[:, t * P:(t + 1) * P], fc2[:, e, c], hid[:, e, c * P:(c + 1) * P],
                             start=(c == 0), stop=(c == HC - 1))
                ins.then_inc(S["fc2_done"], 1)

            def next_layer(g):
                pe.wait_ge(S["yT_ready"], g + 1)
                dst = take("next_layer", g)
                for t in range(TG):
                    ins = mm(dst[:, t * P:(t + 1) * P], kT[:, g, t * P:(t + 1) * P], wnext[:],
                             start=True, stop=True)
                ins.then_inc(S["next_done"], 1)

            return (tokens, turn_input, project_qk, project_v, scores, turn_probs, attend, turn_attn, attn_out,
                    turn_mlp, mlp_up, fold_sums, turn_hidden, mlp_down, turn_ffn, ffn_tokens, expert_up,
                    expert_down, next_layer)

        deal_banks(pe_stages())

        @block.tensor
        def _(pe):
            for stage, n in in_order(pe_stages()):
                stage(n)

        @block.sync
        def _(sp):
            def load_pixels(g):
                for i in range(XH):
                    part = slice(i * KC // XH, (i + 1) * KC // XH)
                    sp.dma_start(x_sb[:, g, part], xT[g, :, part]).then_inc(s_x[g][i], 16)

            sp.dma_start(tokw[:], tok_wT).then_inc(s_tokw, 16)
            load_pixels(0)
            sp.dma_start(row_sb[:], rows.to_broadcast([P, NROW])).then_inc(s_row, 16)
            sp.dma_start(col_sb[:], cols).then_inc(s_col, 16)
            sp.dma_start(qkvo[:], qkvoT).then_inc(s_qkvo, 16)
            for g in range(1, G):
                load_pixels(g)
            sp.dma_start(w2[:], w2T).then_inc(s_w2, 16)
            sp.dma_start(w1[:], w1T).then_inc(s_w1, 16)

            def spread_k(g):
                sp.wait_ge(s_zero, g + 1)
                sp.wait_ge(S["kT_ready"], g + 1)
                for s in range(SUB // 2):
                    at = g * TG * NB
                    sp.dma_start(kdiag[s::SUB // 2, at:at + TG * NB, s, :],
                                 kT[s::SUB // 2, g].rearrange("p (b n) -> p b n", n=N)).then_inc(s_kdiag[g], 16)

            def store(g):
                sp.wait_ge(S["out_ready"], g + 1)
                sp.dma_start(out[g], scratch(g)).then_inc(S["stored"], 16)

            for g in range(G):
                spread_k(g)
            sp.dma_start(wattn[:], attnT).then_inc(s_wan, 16)
            sp.dma_start(wnext[:], nextT).then_inc(s_wan, 16)
            for e in range(TILES):
                sp.dma_start(fc1[:, e], fc1T[e]).then_inc(s_fc[e], 16)
                sp.dma_start(fc2[:, e], fc2T[e]).then_inc(s_fc[e], 16)
            for g in range(G):
                store(g)
            sp.wait_ge(S["stored"], 16 * G)

        @block.gpsimd
        def _(pool):
            def inverse_root(k, g, n):
                pool.wait_ge(s_var[k], g + 1)
                nc.gpsimd.tensor_tensor(rstd[:, k, g, 0:n], var[:, k, g, 0:n], exponent[:, 0:n], ALU.pow)\
                  .then_inc(s_rstd[k], 1)
                pool.wait_ge(s_rstd[k], g + 1)

            def constants(n):
                nc.gpsimd.memset(exponent[:], -0.5).then_inc(s_half, 1)
                nc.gpsimd.memset(ident[:], 0.0).then_inc(s_ident0, 1)
                pool.wait_ge(s_ident0, 1)
                nc.gpsimd.affine_select(out=ident[:], in_=ident[:], compare_op=ALU.not_equal, fill=1.0, base=0,
                                        pattern=[[-1, P]], channel_multiplier=1).then_inc(s_ident, 1)
                nc.gpsimd.memset(ones[:], 1.0).then_inc(s_ones, 1)
                for g in range(G):
                    at = g * TG * NB
                    nc.gpsimd.memset(kdiag[:, at:at + TG * NB], 0.0).then_inc(s_zero, 1)
                nc.gpsimd.memset(vdiag[:], 0.0).then_inc(s_zero, 1)
                pool.wait_ge(s_zero, G + 1)
                for j in range(2):
                    nc.gpsimd.memset(vdiag[j * N:(j + 1) * N, :, :, j, 2 * HD:VC], 1.0).then_inc(s_ones, 1)
                    pool.wait_ge(s_ones, j + 2)
                pool.wait_ge(s_half, 1)

            def root0(g):
                inverse_root(0, g, 2 * TG)

            def root1(g):
                inverse_root(1, g, TG * HEADS)

            def root2(g):
                inverse_root(2, g, TG)

            def root3(g):
                inverse_root(3, g, TG)

            def root4(g):
                inverse_root(4, g, TG)

            def root5(g):
                inverse_root(5, g, 2 * TG)

            def sums(g):
                pool.wait_ge(s_w2rows, 1)
                pool.wait_ge(S["h_ready"], g + 1)
                nc.gpsimd.tensor_tensor(of_group(hsum, g), of_group(h0, g), of_group(h, g), ALU.add)\
                  .then_inc(S["hsum_ready"], 1)
                pool.wait_ge(S["hsum_ready"], 2 * g + 1)
                nc.gpsimd.tensor_tensor(of_group(hsum, g), of_group(hsum, g), over_tiles(mlp_row[:]), ALU.add)\
                  .then_inc(S["hsum_ready"], 1)
                pool.wait_ge(S["hsum_ready"], 2 * g + 2)

            for stage, n in in_order((constants, root0, root1, root2, root3, root4, root5, sums)):
                stage(n)

        @block.scalar
        def _(act):
            def affine(dst, src, w, b):
                return nc.scalar.activation(dst, src, ACT.Identity, scale=w, bias=b)

            def lam_exps(n):
                act.wait_ge(s_lamdot, 1)
                nc.scalar.activation(lam_exp[:], lam_dot[:], ACT.Exp).then_inc(s_lamexp, 1)
                act.wait_ge(s_col, 16)
                nc.scalar.activation(sub_scale[:], col("subln_w"), ACT.Copy, scale=1.0 - LAMBDA_INIT)\
                  .then_inc(s_subs, 1)

            def input_affine(g):
                act.wait_ge(S["xcT_done"], g + 1)
                affine(xnT[:, g], bank_of["turn_input", g, 0][:, 0:COLS], col("n1_w"), col("n1_b"))\
                    .then_inc(S["xnT_ready"], 1)

            def qk_out(g):
                act.wait_ge(S["qk_done"], g + 1)
                src = bank_of["project_qk", g, 0]
                nc.scalar.activation(kT[:, g], src[:, COLS:2 * COLS], ACT.Copy).then_inc(S["kT_ready"], 1)
                nc.scalar.activation(qT[:, g], src[:, 0:COLS], ACT.Copy, scale=HD ** -0.5)\
                  .then_inc(S["qT_ready"], 1)

            def exponentials(t):
                act.wait_ge(S["shifted"], t + 1)
                nc.scalar.activation(prob[:, t % 2], prob[:, t % 2], ACT.Exp).then_inc(S["exp_done"], 1)

            def probs_out(t):
                act.wait_ge(S["probT_done"], t + 1)
                if t >= 2:
                    act.wait_ge(S["o_done"], t - 1)
                nc.scalar.activation(probT[:, t % 2], turned_ps[:], ACT.Copy).then_inc(S["probT_ready"], 1)

            def attn_affine(g):
                if g == 0:
                    act.wait_ge(s_subs, 1)
                act.wait_ge(S["aT_done"], g + 1)
                nc.scalar.activation(xnT[:, g], bank_of["turn_attn", g, 0][:, 0:COLS], ACT.Copy,
                                     scale=sub_scale[:]).then_inc(S["aT_ready"], 1)

            def mlp_affine(g):
                act.wait_ge(S["zcT_done"], g + 1)
                affine(qT[:, g], bank_of["turn_mlp", g, 0][:, 0:COLS], col("mln1_w"), col("mln1_b"))\
                    .then_inc(S["zT_ready"], 1)

            def mlp_gelu(t):
                act.wait_ge(S["w1_read"], t + 1)
                nc.scalar.activation(hid[:, t], hid[:, t], ACT.Gelu).then_inc(S["gelu_ready"], 1)

            def hidden_out(g):
                for i in range(2):
                    act.wait_ge(S["hidT_done"], 2 * g + i + 1)
                    nc.scalar.activation(hidT[:, g, 2 * i:2 * i + 2],
                                         bank_of["turn_hidden", g, i][:].rearrange("p (c n) -> p c n", c=2),
                                         ACT.Copy).then_inc(S["hidT_ready"], 1)

            def ffn_affine(g):
                act.wait_ge(S["nT_done"], g + 1)
                affine(xnT[:, g], bank_of["turn_ffn", g, 0][:, 0:COLS], col("ln_g"), col("ln_b"))\
                    .then_inc(S["nT_ready"], 1)

            def ffn_tokens_out(g):
                act.wait_ge(S["xa_done"], g + 1)
                nc.scalar.activation(qT[:, g], bank_of["ffn_tokens", g, 0][:, 0:COLS], ACT.Identity,
                                     bias=col("attn_b")).then_inc(S["xaT_ready"], 1)

            def expert_gelu(e):
                act.wait_ge(S["fc1_done"], e + 1)
                for c in range(HC):
                    part = slice(c * P, (c + 1) * P)
                    ins = nc.scalar.activation(hid[:, e, part], bank_of["expert_up", e, 0][:, part], ACT.Gelu,
                                               bias=col("fc1_b", e * HC + c))
                ins.then_inc(S["fgelu_ready"], 1)

            def last_gelu(g):
                act.wait_ge(S["next_read"], g + 1)
                nc.scalar.activation(scratch(g), scratch(g), ACT.Gelu).then_inc(S["ngelu_ready"], 1)

            for stage, n in in_order((lam_exps, input_affine, qk_out, exponentials, probs_out, attn_affine,
                                      mlp_affine, mlp_gelu, hidden_out, ffn_affine, ffn_tokens_out, expert_gelu,
                                      last_gelu)):
                stage(n)

        @block.vector
        def _(dve):
            steps = [0]

            def step(ins):
                steps[0] += 1
                ins.then_inc(s_dve, 1)
                return steps[0]

            def settle():
                dve.wait_ge(s_dve, steps[0])

            def moments(k, g, src):
                for t in range(TG):
                    step(nc.vector.bn_stats(stats[:, k, t], src[:, t]))
                settle()
                for t in range(TG):
                    step(nc.vector.bn_aggr(mv[:, k, g, t], stats[:, k, t]))
                settle()

            def shifted_variance(k, norm, g):
                nc.vector.tensor_scalar(var[:, norm, g, 0:TG], mv[:, k, g, :, 1], EPS, None, ALU.add)\
                  .then_inc(s_var[norm], 1)

            def double_variance(k, norm, g):
                step(nc.vector.tensor_scalar(var[:, norm, g, TG:2 * TG], mv[:, k, g, :, 1], 1.0 + EPS, EPS * EPS,
                                             ALU.mult, ALU.add))
                nc.vector.tensor_scalar(var[:, norm, g, 0:TG], mv[:, k, g, :, 1], EPS, None, ALU.add)\
                  .then_inc(s_var[norm], 1)

            def normalise(dst, src, k, norm, g, second=0):
                for t in range(TG):
                    ins = nc.vector.tensor_scalar(dst[:, t], src[:, t], mv[:, k, g, t, 0:1],
                                                  rstd[:, norm, g, second * TG + t:second * TG + t + 1],
                                                  ALU.subtract, ALU.mult)
                return ins

            def add(dst, a, b):
                return nc.vector.tensor_tensor(dst, a, b, ALU.add)

            def lam_dots(n):
                dve.wait_ge(s_row, 16)
                q1k1q2k2 = row("lam").rearrange("p (a b d) -> p a b d", a=2, b=2)
                step(nc.vector.tensor_tensor(lam_prod[:], q1k1q2k2[:, :, 0], q1k1q2k2[:, :, 1], ALU.mult))
                settle()
                nc.vector.tensor_reduce(lam_dot[:], lam_prod[:], AX, ALU.add).then_inc(s_lamdot, 1)

            def lam(n):
                dve.wait_ge(s_lamexp, 1)
                step(nc.vector.tensor_tensor(lam_diff[:], lam_exp[:, 1:2], lam_exp[:, 0:1], ALU.subtract))
                settle()
                step(nc.vector.tensor_scalar(neg_lam[:], lam_diff[:], -LAMBDA_INIT, None, ALU.add))

            def fold_weights(n):
                dve.wait_ge(s_w2, 16)
                dve.wait_ge(s_col, 16)
                at = COL["mln2_w"][0]
                nc.vector.tensor_tensor(w2n[:], w2[:], col_sb[:, at:at + HC][:, :, None].to_broadcast([P, HC, P]),
                                        ALU.mult)
                at = COL["mln2_b"][0]
                nc.vector.tensor_copy(mln2_b[:], col_sb[:, at:at + HC][:, :, None].to_broadcast([P, HC, P]))\
                  .then_inc(s_w2n, 1)

            def fold_rows(n):
                dve.wait_ge(s_w2sums, 1)
                src = bank_of["fold_sums", 0, 0]
                step(nc.vector.tensor_copy(w2n_sums[:], src[:, 0:P]))
                add(mlp_row[:], src[:, P:2 * P], row("mb2")).then_inc(s_w2rows, 1)

            def embedding(g):
                dve.wait_ge(S["tok_done"], g + 1)
                add(of_group(h0, g), tiled(bank_of["tokens", g, 0]), over_tiles(row("tok_b")))\
                    .then_inc(S["h0_ready"], 1)
                dve.wait_ge(S["h0_ready"], g + 1)
                moments(0, g, of_group(h0, g))
                double_variance(0, 0, g)

            def input_norm(g):
                dve.wait_ge(s_rstd[0], g + 1)
                normalise(of_group(cent, g), of_group(h0, g), 0, 0, g, second=1).then_inc(S["xc_ready"], 1)
                step(normalise(of_group(xin, g), of_group(h0, g), 0, 0, g))
                settle()
                step(add(of_group(xin, g), of_group(xin, g), over_tiles(row("n2_b"))))

            def values(g):
                if g == 0:
                    dve.wait_ge(s_zero, G + 1)
                dve.wait_ge(S["v_done"], g + 1)
                src = bank_of["project_v", g, 0][:].rearrange("p (b h d) -> p b h d", h=HEADS, d=2 * HD)
                at = g * TG * NB
                for j in range(2):
                    half = slice(j * N, (j + 1) * N)
                    ins = nc.vector.tensor_copy(vdiag[half, at:at + TG * NB, :, j, 0:2 * HD], src[half])
                ins.then_inc(S["vdiag_ready"], 1)

            def softmax_shift(t):
                dve.wait_ge(S["s_done"], t + 1)
                step(nc.vector.tensor_reduce(negmax[:, t % 2], score_ps[:], AX, ALU.max, negate=True))
                settle()
                if t >= 2:
                    dve.wait_ge(S["probT_done"], t - 1)
                add(prob[:, t % 2], score_ps[:], negmax[:, t % 2][:, :, None].to_broadcast([P, SUB, N]))\
                    .then_inc(S["shifted"], 1)

            def difference(t):
                dve.wait_ge(S["o_done"], t + 1)
                step(nc.vector.reciprocal(rden[:, t % 2], value_ps[:, :, :, 2 * HD]))
                settle()
                step(nc.vector.tensor_scalar(rden[:, t % 2, :, 1], rden[:, t % 2, :, 1], neg_lam[:], None, ALU.mult))
                settle()
                nc.vector.tensor_tensor(onorm[:, t % 2], value_ps[:, :, :, 0:2 * HD],
                                        rden[:, t % 2][:, :, :, None].to_broadcast([P, HEADS, 2, 2 * HD]),
                                        ALU.mult).then_inc(S["o_read"], 1)
                dve.wait_ge(S["o_read"], t + 1)
                step(add(attn[:, t], onorm[:, t % 2, :, 0], onorm[:, t % 2, :, 1]))

            def rms(g):
                settle()
                a = of_group(attn, g).rearrange("p t h d -> p (t h) d")
                sq = scratch(g).rearrange("p t (h d) -> p (t h) d", d=2 * HD)
                step(nc.vector.tensor_tensor(sq, a, a, ALU.mult))
                settle()
                step(nc.vector.tensor_reduce(var[:, 1, g], sq, AX, ALU.add))
                settle()
                nc.vector.tensor_scalar(var[:, 1, g], var[:, 1, g], 1.0 / (2 * HD), EPS, ALU.mult, ALU.add)\
                  .then_inc(s_var[1], 1)

            def rms_apply(g):
                dve.wait_ge(s_rstd[1], g + 1)
                a = of_group(attn, g).rearrange("p t h d -> p (t h) d")
                nc.vector.tensor_tensor(of_group(cent, g).rearrange("p t (h d) -> p (t h) d", d=2 * HD), a,
                                        rstd[:, 1, g][:, :, None].to_broadcast([P, TG * HEADS, 2 * HD]), ALU.mult)\
                  .then_inc(S["rms_ready"], 1)

            def second_moments(g):
                dve.wait_ge(S["wo_done"], g + 1)
                moments(1, g, tiled(bank_of["attn_out", g, 0]))
                shifted_variance(1, 2, g)

            def residual(g):
                dve.wait_ge(s_rstd[2], g + 1)
                src = tiled(bank_of["attn_out", g, 0])
                for t in range(TG):
                    step(nc.vector.scalar_tensor_tensor(scratch(g)[:, t], src[:, t], mv[:, 1, g, t, 0:1],
                                                        row("n2_w"), ALU.subtract, ALU.mult))
                settle()
                for t in range(TG):
                    ins = nc.vector.scalar_tensor_tensor(of_group(h, g)[:, t], scratch(g)[:, t],
                                                         rstd[:, 2, g, t:t + 1], of_group(xin, g)[:, t],
                                                         ALU.mult, ALU.add)
                ins.then_inc(S["h_ready"], 1)
                dve.wait_ge(S["h_ready"], g + 1)
                moments(2, g, of_group(h, g))
                shifted_variance(2, 3, g)

            def mlp_norm(g):
                dve.wait_ge(s_rstd[3], g + 1)
                normalise(of_group(cent, g), of_group(h, g), 2, 3, g).then_inc(S["zc_ready"], 1)

            def mlp_bias(t):
                dve.wait_ge(S["w1_done"], t + 1)
                add(hid[:, t], bank_of["mlp_up", t, 0][:], row("mb1")).then_inc(S["w1_read"], 1)

            def hidden_moments(g):
                dve.wait_ge(S["gelu_ready"], (g + 1) * TG)
                moments(3, g, of_group(hid, g))
                shifted_variance(3, 4, g)

            def mlp_result(g):
                dve.wait_ge(s_rstd[4], g + 1)
                step(nc.vector.scalar_tensor_tensor(nmr[:, g], mv[:, 3, g, :, 0], -1.0, rstd[:, 4, g, 0:TG],
                                                    ALU.mult, ALU.mult))
                settle()
                dve.wait_ge(S["hsum_ready"], 2 * (g + 1))
                for t in range(TG):
                    step(nc.vector.scalar_tensor_tensor(of_group(hsum, g)[:, t], w2n_sums[:], nmr[:, g, t:t + 1],
                                                        of_group(hsum, g)[:, t], ALU.mult, ALU.add))
                settle()
                dve.wait_ge(S["w2_done"], g + 1)
                src = tiled(bank_of["mlp_down", g, 0])
                for t in range(TG):
                    ins = nc.vector.scalar_tensor_tensor(of_group(h1, g)[:, t], src[:, t], rstd[:, 4, g, t:t + 1],
                                                         of_group(hsum, g)[:, t], ALU.mult, ALU.add)
                ins.then_inc(S["h1_ready"], 1)
                dve.wait_ge(S["h1_ready"], g + 1)
                moments(4, g, of_group(h1, g))
                double_variance(4, 5, g)

            def ffn_norm(g):
                dve.wait_ge(s_rstd[5], g + 1)
                normalise(of_group(cent, g), of_group(h1, g), 4, 5, g, second=1)
                normalise(of_group(xin, g), of_group(h1, g), 4, 5, g).then_inc(S["n_ready"], 1)

            def expert_out(g):
                dve.wait_ge(S["fc2_done"], (g + 1) * TG)
                at = COL["fc2_b"][0] + g * TG
                add(tiled(kT[:, g]), tiled(bank_of["expert_down", g * TG, 0]),
                    col_sb[:, at:at + TG][:, :, None].to_broadcast([P, TG, P])).then_inc(S["yT_ready"], 1)

            def next_bias(g):
                dve.wait_ge(S["next_done"], g + 1)
                add(scratch(g), tiled(bank_of["next_layer", g, 0]), over_tiles(row("next_b")))\
                    .then_inc(S["next_read"], 1)

            def output(g):
                dve.wait_ge(S["ngelu_ready"], g + 1)
                add(scratch(g), scratch(g), of_group(h1, g)).then_inc(S["out_ready"], 1)

            for stage, n in in_order((lam_dots, lam, fold_weights, fold_rows, embedding, input_norm, values,
                                      softmax_shift, difference, rms, rms_apply, second_moments, residual, mlp_norm,
                                      mlp_bias, hidden_moments, mlp_result, ffn_norm, expert_out, next_bias, output)):
                stage(n)


def kernel(x, L0_tok_w, L0_tok_b, L0_attn_Wq, L0_attn_Wk, L0_attn_Wv, L0_attn_Wo, L0_attn_lq1, L0_attn_lk1,
           L0_attn_lq2, L0_attn_lk2, L0_attn_subln_w, L0_attn_n1_w, L0_attn_n1_b, L0_attn_n2_w, L0_attn_n2_b,
           L0_attn_mln1_w, L0_attn_mln1_b, L0_attn_mW1, L0_attn_mb1, L0_attn_mln2_w, L0_attn_mln2_b, L0_attn_mW2,
           L0_attn_mb2, L0_ffn_ln_g, L0_ffn_ln_b, L0_ffn_attn_w, L0_ffn_attn_b, L0_ffn_gate_w, L0_ffn_fc1_w,
           L0_ffn_fc1_b, L0_ffn_fc2_w, L0_ffn_fc2_b, L0_ffn_next_w, L0_ffn_next_b):
    import numpy as np
    import concourse.bacc as bacc
    from concourse.bass_utils import run_bass_kernel_spmd

    def vectors(a):
        return np.asarray(a).reshape(-1, P).T

    def maps_last(w):
        return np.asarray(w).reshape(2, SUB // 2, HD, P).transpose(3, 0, 2, 1).reshape(P, P)

    side = np.asarray(x).shape[2] // 16
    px = np.asarray(x).reshape(NB, G, TG, 3, side, 16, side, 16).transpose(3, 5, 7, 1, 2, 0, 4, 6)
    px = px.reshape(KC, P, G, COLS).transpose(2, 1, 0, 3)
    columns = {"n1_w": L0_attn_n1_w, "n1_b": L0_attn_n1_b, "subln_w": np.tile(np.asarray(L0_attn_subln_w), HEADS),
               "mln1_w": L0_attn_mln1_w, "mln1_b": L0_attn_mln1_b, "mln2_w": L0_attn_mln2_w,
               "mln2_b": L0_attn_mln2_b, "ln_g": L0_ffn_ln_g, "ln_b": L0_ffn_ln_b, "attn_b": L0_ffn_attn_b,
               "fc1_b": L0_ffn_fc1_b, "fc2_b": L0_ffn_fc2_b}
    lam = np.concatenate([np.asarray(v) for v in (L0_attn_lq1, L0_attn_lk1, L0_attn_lq2, L0_attn_lk2)])
    rows = {"tok_b": L0_tok_b, "n2_w": L0_attn_n2_w, "n2_b": L0_attn_n2_b, "mb2": L0_attn_mb2,
            "next_b": L0_ffn_next_b, "mb1": L0_attn_mb1, "lam": lam}
    arrays = {
        "xT": px,
        "tok_wT": np.asarray(L0_tok_w).T.reshape(KC, P, P).transpose(1, 0, 2),
        "cols": np.concatenate([vectors(columns[n]) for n in COL], axis=1),
        "rows": np.concatenate([np.asarray(rows[n]).reshape(1, -1) for n in ROW], axis=1),
        "qkvoT": np.stack([maps_last(L0_attn_Wq), maps_last(L0_attn_Wk), np.asarray(L0_attn_Wv).T,
                           np.asarray(L0_attn_Wo).T], axis=1),
        "w1T": np.asarray(L0_attn_mW1).T,
        "w2T": np.asarray(L0_attn_mW2).T.reshape(HC, P, P).transpose(1, 0, 2),
        "attnT": np.asarray(L0_ffn_attn_w).T,
        "nextT": np.asarray(L0_ffn_next_w).T,
        "fc1T": np.asarray(L0_ffn_fc1_w).transpose(0, 2, 1),
        "fc2T": np.asarray(L0_ffn_fc2_w).transpose(0, 2, 1).reshape(TILES, HC, P, P).transpose(0, 2, 1, 3),
    }
    arrays = {k: np.ascontiguousarray(v) for k, v in arrays.items()}
    nc = bacc.Bacc("TRN2", target_bir_lowering=False, num_devices=1)
    args = [nc.dram_tensor(n, a.shape, mybir.dt.from_np(a.dtype), kind="ExternalInput").ap() for n, a in arrays.items()]
    out = nc.dram_tensor("out", (G, P, TG, P), mybir.dt.float32, kind="ExternalOutput").ap()
    vit_layer(nc, *args, out)
    r = run_bass_kernel_spmd(nc, [arrays], core_ids=[0])
    y = r.results[0]["out"].reshape(G, NB, N, TG, P).transpose(1, 0, 3, 2, 4)
    return np.ascontiguousarray(y.reshape(NB * G * TG, N, P))
```

```python
import concourse.bass as bass
from concourse import mybir
from contextlib import ExitStack

P = 128
TILES = 8
G = 4
TG = TILES // G
COLS = TG * P
KC = 6
HEADS = 8
HD = 8
NB = 2
N = 64
SUB = 2 * HEADS
VC = 2 * HD + 1
OH = 128
HC = 4
HID = HC * P
PARTS = 3
EPS = 1e-5
LAMBDA_INIT = 0.8 - 0.6 * 1.0

COL = {}
for _name, _n in (("n1_w", 1), ("n1_b", 1), ("subln_w", 1), ("mln1_w", 1), ("mln1_b", 1), ("mln2_w", HC),
                  ("mln2_b", HC), ("mb1", HC), ("ln_g", 1), ("ln_b", 1), ("attn_b", 1), ("fc1_b", TILES * HC),
                  ("fc2_b", TILES)):
    COL[_name] = sum(n for _, n in COL.values()), _n
NCOL = sum(n for _, n in COL.values())
ROW = {}
for _name, _n in (("tok_b", P), ("n2_w", P), ("n2_b", P), ("mb2", P), ("lam", 4 * HD), ("next_b", P)):
    ROW[_name] = sum(n for _, n in ROW.values()), _n
NROW = sum(n for _, n in ROW.values())


START = {
    "tokens": [0, 1, 4, 5],
    "turn_input": [2, 6, 9, 12],
    "project_qk": [3, 8, 11, 18],
    "project_v": [7, 13, 22, 37],
    "scores": [10, 14, 17, 21, 25, 28, 33, 36],
    "fold_sums": [15],
    "turn_probs": [16, 19, 24, 27, 32, 35, 39, 42],
    "attend": [20, 23, 26, 30, 34, 38, 41, 44],
    "turn_attn": [29, 40, 45, 50],
    "attn_out": [31, 43, 47, 52],
    "turn_mlp": [46, 51, 56, 58],
    "mlp_up": [48, 49, 53, 54, 57, 59, 60, 62],
    "mlp_down": [55, 61, 64, 67],
    "turn_ffn": [63, 68, 77, 79],
    "ffn_tokens": [65, 70, 81, 82],
    "expert_up": [66, 69, 72, 73, 83, 84, 85, 86],
    "expert_down": [71, 74, 75, 76, 87, 88, 89, 90],
    "next_layer": [78, 80, 91, 92],
    "constants": [0],
    "clear_k": [1, 3, 10, 11],
    "clear_v": [2],
    "root0": [4, 5, 7, 9],
    "skip_input": [6, 8, 14, 16],
    "root1": [12, 13, 15, 18, 20, 22, 24, 25],
    "root2": [17, 23, 27, 29],
    "root3": [21, 26, 28, 32],
    "sums": [30, 31, 34, 40],
    "root4": [33, 36, 38, 39],
    "root5": [35, 37, 41, 42],
    "input_affine": [0, 2, 3, 10],
    "qk_out": [1, 4, 6, 13],
    "values": [5, 7, 17, 31],
    "exponentials": [8, 12, 16, 18, 24, 25, 30, 34],
    "probs_out": [9, 15, 20, 21, 26, 28, 32, 36],
    "lam_exps": [11],
    "attn_square": [14, 19, 22, 27, 29, 33, 37, 39],
    "attn_affine": [23, 35, 38, 43],
    "mlp_affine": [40, 44, 51, 52],
    "mlp_gelu": [41, 45, 47, 49, 53, 54, 56, 59],
    "hidden_square": [42, 46, 48, 50, 55, 57, 60, 61],
    "ffn_affine": [58, 64, 69, 70],
    "ffn_tokens_out": [62, 66, 73, 74],
    "expert_gelu": [63, 65, 67, 68, 75, 76, 77, 78],
    "last_gelu": [71, 72, 79, 80],
    "embedding": [0, 2, 5, 7],
    "input_norm": [1, 3, 6, 8],
    "lam_dots": [4],
    "softmax_shift": [9, 11, 13, 16, 20, 25, 28, 33],
    "fold_weights": [10],
    "lam": [12],
    "difference": [14, 17, 21, 27, 29, 34, 38, 43],
    "fold_rows": [15],
    "rms": [18, 19, 24, 31, 32, 37, 42, 45],
    "rms_apply": [22, 23, 30, 35, 40, 41, 48, 50],
    "second_moments": [26, 39, 47, 52],
    "residual": [36, 46, 51, 55],
    "mlp_norm": [44, 49, 53, 57],
    "sum_squares": [54, 59, 62, 65],
    "hidden_stats": [56, 61, 64, 67],
    "mlp_result": [58, 63, 68, 69],
    "ffn_norm": [60, 66, 70, 72],
    "expert_out": [71, 73, 76, 77],
    "output": [74, 75, 78, 79],
    "split_row": [19],
}


def in_order(stages):
    turns = [(at, i, stage, n) for i, stage in enumerate(stages) for n, at in enumerate(START[stage.__name__])]
    for _, _, stage, n in sorted(turns, key=lambda x: x[:2] + x[3:]):
        yield stage, n


def vit_layer(nc, xT, tok_wT, cols, rows, qkvoT, w1T, w2T, attnT, nextT, fc1T, fc2T, out):
    fp32 = mybir.dt.float32
    bf16 = mybir.dt.bfloat16
    ALU = mybir.AluOpType
    ACT = mybir.ActivationFunctionType
    AX = mybir.AxisListType.X

    ctx = ExitStack()
    with ctx:
        def sb(name, shape, dtype=fp32):
            return ctx.enter_context(nc.sbuf_tensor(name, shape, dtype))

        def sem(name):
            return ctx.enter_context(nc.semaphore(name))

        x_sb = sb("x_sb", [P, G, KC, COLS])
        tokw = sb("tokw", [P, KC, P])
        col_sb = sb("col_sb", [P, NCOL])
        row_sb = sb("row_sb", [P, NROW])
        qkvo = sb("qkvo", [P, 4, P])
        w1 = sb("w1", [P, HID])
        w2 = sb("w2", [P, HC, P])
        w2n = sb("w2n", [P, HC, P + 1])
        wattn = sb("wattn", [P, P])
        wnext = sb("wnext", [P, P])
        fc1 = sb("fc1", [P, TILES, HID])
        fc2 = sb("fc2", [P, TILES, HC, P])
        ident = sb("ident", [P, P])
        ones = sb("ones", [P, P])
        mln2_b = sb("mln2_b", [P, HC, P])
        w2n_sums = sb("w2n_sums", [P, P])
        mlp_row = sb("mlp_row", [P, P])
        exponent = sb("exponent", [P, HEADS])
        ones16 = sb("ones16", [PARTS, P], bf16)
        bias16 = sb("bias16", [PARTS, P], bf16)
        parts = sb("parts", [1, PARTS, P], bf16)
        rest = sb("rest", [1, PARTS - 1, P])
        sub_scale = sb("sub_scale", [P, 1])
        lam_prod = sb("lam_prod", [P, 2, HD])
        lam_dot = sb("lam_dot", [P, 2])
        lam_exp = sb("lam_exp", [P, 2])
        lam_diff = sb("lam_diff", [P, 1])
        neg_lam = sb("neg_lam", [P, 1])
        h0 = sb("h0", [P, TILES, P])
        xin = sb("xin", [P, TILES, P])
        cent = sb("cent", [P, TILES, P])
        h = sb("h", [P, TILES, P])
        hsum = sb("hsum", [P, TILES, P])
        h1 = sb("h1", [P, TILES, P])
        hid = sb("hid", [P, TILES, HID])
        xnT = sb("xnT", [P, G, COLS])
        qT = sb("qT", [P, G, COLS])
        kT = sb("kT", [P, G, COLS])
        hidT = x_sb[:, :, 0:HC]
        kdiag = sb("kdiag", [P, TILES * NB, SUB // 2, N])
        vdiag = sb("vdiag", [P, TILES * NB, HEADS, 2, VC])
        prob = sb("prob", [P, 2, SUB, N])
        probT = sb("probT", [P, 2, HEADS, P])
        negmax = sb("negmax", [P, 2, SUB])
        rden = sb("rden", [P, 2, HEADS, 2])
        onorm = sb("onorm", [P, 2, HEADS, 2, 2 * HD])
        stats = sb("stats", [P, 5, TG, 6])
        mv = sb("mv", [P, 5, G, TG, 2])
        var = sb("var", [P, 6, G, TG * HEADS])
        rstd = sb("rstd", [P, 6, G, TG * HEADS])
        mean_sq = sb("mean_sq", [P, TG])
        nmr = sb("nmr", [P, G, TG])

        def ps(name, banks):
            return ctx.enter_context(nc.psum_tensor(name, [P, banks * HID], fp32))

        score_banks, turned_banks, value_bank = ps("score_banks", 2), ps("turned_banks", 2), ps("value_bank", 1)
        score_ps = score_banks[:].rearrange("p (s n) -> p s n", n=N)
        turned_ps = turned_banks[:].rearrange("p (h n) -> p h n", n=P)
        value_ps = value_bank[:, 0:HEADS * 2 * VC].rearrange("p (h j c) -> p h j c", h=HEADS, j=2)
        ring = [ps(f"ring{i}", 1) for i in range(3)]

        def col(name, i=0):
            at = COL[name][0] + i
            return col_sb[:, at:at + 1]

        def row(name):
            at, n = ROW[name]
            return row_sb[:, at:at + n]

        def over_tiles(ap):
            return ap[:, None, :].to_broadcast([P, TG, ap.shape[1]])

        def tiled(ap):
            return ap[:, 0:COLS].rearrange("p (t n) -> p t n", n=P)

        def of_group(t, g):
            return t[:, g * TG:(g + 1) * TG]

        def scratch(g):
            return tiled(x_sb[:, g, HC])

        def attn(t):
            at = (t % TG) * P
            return x_sb[:, t // TG, HC + 1, at:at + P].rearrange("p (h d) -> p h d", d=2 * HD)

        def square_sums(g):
            return x_sb[:, g, HC + 1]

        def squares(t):
            return scratch(t // TG)[:, t % TG]

        s_col, s_row, s_tokb, s_qkvo = sem("cols_in"), sem("rows_in"), sem("tok_b_in"), sem("qkvo_in")
        XH = 3
        s_tokw = [sem(f"tokw_in_{i}") for i in range(XH)]
        s_x = [[sem(f"x_in_{g}_{i}") for i in range(XH)] for g in range(G)]
        s_w1, s_w2, s_wan = sem("w1_in"), sem("w2_in"), sem("wattn_wnext_in")
        s_fc = [sem(f"fc_in_{e}") for e in range(TILES)]
        s_kdiag = [sem(f"kdiag_ready_{g}") for g in range(G)]
        s_ident0, s_ident, s_half = sem("ident_cleared"), sem("ident_ready"), sem("exponent_ready")
        s_kzero, s_vzero, s_ones = sem("kdiag_cleared"), sem("vdiag_cleared"), sem("ones_ready")
        s_parts, s_bias = sem("bias_parts"), sem("bias16_in")
        s_lamdot, s_lamexp, s_subs = sem("lam_dots"), sem("lam_exps"), sem("sub_scale_ready")
        s_w2n, s_w2sums, s_w2rows = sem("w2n_ready"), sem("w2n_sums_done"), sem("mlp_rows_ready")
        s_dve = sem("vector_steps")
        s_var = [sem(f"var_ready_{k}") for k in range(6)]
        s_rstd = [sem(f"rstd_ready_{k}") for k in range(6)]
        names = ("tok_done h0_ready xin_ready xc_ready xcT_done xnT_ready qk_done kT_ready qT_ready "
                 "v_done vdiag_ready s_done shifted exp_done probT_done probT_ready o_done o_read attn_ready "
                 "squared rms_ready aT_done aT_ready wo_done h_ready hsum_ready zc_ready zcT_done zT_ready w1_done gelu_ready "
                 "zsq_ready sumsq_ready w2_done h1_ready n_ready nT_done nT_ready xa_done xaT_ready fc1_done "
                 "fgelu_ready fc2_done yT_ready next_done ngelu_ready out_ready stored").split()
        S = {n: sem(n) for n in names}

        block = ctx.enter_context(nc.Block())

        RING_USES = {"tokens": "h0_ready", "turn_input": "xnT_ready", "project_qk": "qT_ready",
                     "project_v": "vdiag_ready", "turn_attn": "aT_ready", "attn_out": "h_ready",
                     "turn_mlp": "zT_ready", "mlp_up": "gelu_ready",
                     "mlp_down": "h1_ready", "turn_ffn": "nT_ready", "ffn_tokens": "xaT_ready",
                     "expert_up": "fgelu_ready", "expert_down": "yT_ready", "next_layer": "ngelu_ready",
                     "fold_sums": "mlp_rows_ready"}
        bank_of, readers_before = {}, {}

        def deal_banks(stages):
            last, used, turn, banks = [None] * len(ring), [-1] * len(ring), 0, list(ring)
            for stage, n in in_order(stages):
                name = stage.__name__
                if name == "attend" and n == TILES - 1:
                    banks += [score_banks[:, 0:HID], score_banks[:, HID:2 * HID], turned_banks[:, 0:HID],
                              turned_banks[:, HID:2 * HID]]
                    used += [-1] * 4
                    last += [(S["shifted"], TILES)] * 2 + [(S["probT_ready"], TILES)] * 2
                if name not in RING_USES or (name == "expert_down" and n % TG):
                    continue
                reader = s_w2rows if name == "fold_sums" else S[RING_USES[name]]
                b = min(range(len(banks)), key=lambda i: used[i])
                count = n // TG + 1 if name == "expert_down" else n + 1
                bank_of[name, n], readers_before[name, n] = banks[b], last[b]
                last[b], used[b], turn = (reader, count), turn, turn + 1

        def pe_stages():
            mm = nc.tensor.matmul
            pe = nc.tensor

            def turn(dst, src):
                return nc.tensor.transpose(dst, src, ident[:])

            def take(name, n):
                if readers_before[name, n]:
                    pe.wait_ge(*readers_before[name, n])
                return bank_of[name, n]

            def turn_group(name, src, g):
                dst = take(name, g)
                for t in range(TG):
                    ins = turn(dst[:, t * P:(t + 1) * P], src[:, g * TG + t])
                return ins

            def tokens(g):
                dst = take("tokens", g)
                for c in range(KC):
                    if c % (KC // XH) == 0:
                        if g == 0:
                            pe.wait_ge(s_tokw[c // (KC // XH)], 16)
                        pe.wait_ge(s_x[g][c // (KC // XH)], 16)
                    for t in range(TG):
                        ins = mm(dst[:, t * P:(t + 1) * P], x_sb[:, g, c, t * P:(t + 1) * P], tokw[:, c],
                                 start=(c == 0 and t == 0), stop=(c == KC - 1), skip_group_check=True)
                ins.then_inc(S["tok_done"], 1)

            def turn_input(g):
                if g == 0:
                    pe.wait_ge(s_ident, 1)
                pe.wait_ge(S["xc_ready"], g + 1)
                turn_group("turn_input", cent, g).then_inc(S["xcT_done"], 1)

            def project_qk(g):
                if g == 0:
                    pe.wait_ge(s_qkvo, 16)
                pe.wait_ge(S["xnT_ready"], g + 1)
                dst = take("project_qk", g)
                mm(dst[:, COLS:2 * COLS], qkvo[:, 1], xnT[:, g], start=True, stop=True)
                mm(dst[:, 0:COLS], qkvo[:, 0], xnT[:, g], start=True, stop=True).then_inc(S["qk_done"], 1)

            def project_v(g):
                pe.wait_ge(S["xnT_ready"], g + 1)
                dst = take("project_v", g)
                for b in range(TG * NB):
                    for j in range(2):
                        ins = mm(dst[j * N:(j + 1) * N, b * P:(b + 1) * P], xnT[:, g, b * N:(b + 1) * N],
                                 qkvo[:, 2], start=True, stop=True)
                ins.then_inc(S["v_done"], 1)

            def scores(t):
                g = t // TG
                if t > 0:
                    pe.wait_ge(S["shifted"], t)
                pe.wait_ge(S["qT_ready"], g + 1)
                pe.wait_ge(s_kdiag[g], 16 * SUB // 2)
                for r, b in ((0, 0), (1, 1), (0, 1), (1, 0)):
                    rows_r = slice(64 * r, 64 * r + 64)
                    at = ((t % TG) * NB + b) * N
                    ins = mm(score_ps[b * N:(b + 1) * N, r * SUB // 2:(r + 1) * SUB // 2], qT[rows_r, g, at:at + N],
                             kdiag[rows_r, t * NB + b], start=True, stop=True)
                ins.then_inc(S["s_done"], 1)

            def turn_probs(t):
                pe.wait_ge(S["exp_done"], t + 1)
                if t > 0:
                    pe.wait_ge(S["probT_ready"], t)
                for hd in range(HEADS):
                    ins = turn(turned_ps[:, hd], prob[:, t % 2, 2 * hd:2 * hd + 2].rearrange("p s n -> p (s n)"))
                ins.then_inc(S["probT_done"], 1)

            def attend(t):
                pe.wait_ge(S["probT_ready"], t + 1)
                pe.wait_ge(S["vdiag_ready"], t // TG + 1)
                if t == 0:
                    pe.wait_ge(s_ones, 5)
                else:
                    pe.wait_ge(S["o_read"], t)
                for hd in range(HEADS):
                    for b in range(NB):
                        ins = mm(value_ps[b * N:(b + 1) * N, hd], probT[:, t % 2, hd, b * N:(b + 1) * N],
                                 vdiag[:, t * NB + b, hd], start=True, stop=True)
                ins.then_inc(S["o_done"], 1)

            def turn_attn(g):
                pe.wait_ge(S["rms_ready"], (g + 1) * TG)
                turn_group("turn_attn", cent, g).then_inc(S["aT_done"], 1)

            def attn_out(g):
                pe.wait_ge(S["aT_ready"], g + 1)
                dst = take("attn_out", g)
                for t in range(TG):
                    ins = mm(dst[:, t * P:(t + 1) * P], xnT[:, g, t * P:(t + 1) * P], qkvo[:, 3],
                             start=True, stop=True)
                ins.then_inc(S["wo_done"], 1)

            def turn_mlp(g):
                pe.wait_ge(S["zc_ready"], g + 1)
                turn_group("turn_mlp", cent, g).then_inc(S["zcT_done"], 1)

            def mlp_up(n):
                if n == 0:
                    pe.wait_ge(s_w1, 16)
                pe.wait_ge(S["zT_ready"], n // 2 + 1)
                dst = take("mlp_up", n)
                for c in range(2):
                    at = (2 * (n % 2) + c) * P
                    ins = mm(dst[:, c * COLS:(c + 1) * COLS], w1[:, at:at + P], qT[:, n // 2], start=True, stop=True)
                ins.then_inc(S["w1_done"], 1)

            def fold_sums(n):
                pe.wait_ge(s_w2n, 1)
                pe.wait_ge(s_ones, 2)
                dst = take("fold_sums", 0)
                for c in range(HC):
                    mm(dst[:, 0:P], ones[:], w2n[:, c, 0:P], start=(c == 0), stop=(c == HC - 1))
                for c in range(HC):
                    ins = mm(dst[:, P:2 * P], mln2_b[:, c], w2[:, c], start=(c == 0), stop=(c == HC - 1))
                ins.then_inc(s_w2sums, 1)

            def mlp_down(g):
                if g == 0:
                    pe.wait_ge(s_w2n, 1)
                    pe.wait_ge(s_ones, 3)
                pe.wait_ge(S["gelu_ready"], 2 * (g + 1))
                dst = take("mlp_down", g)
                for t in range(TG):
                    for c in range(HC):
                        mm(dst[:, t * (P + 1):(t + 1) * (P + 1)], hidT[:, g, c, t * P:(t + 1) * P], w2n[:, c],
                           start=(c == 0), stop=(c == HC - 1))
                pe.wait_ge(S["sumsq_ready"], g + 1)
                for t in range(TG):
                    at = TG * (P + 1) + t
                    ins = mm(dst[:, at:at + 1], square_sums(g)[:, t * P:(t + 1) * P], ones[:, 0:1],
                             start=True, stop=True)
                ins.then_inc(S["w2_done"], 1)

            def turn_ffn(g):
                pe.wait_ge(S["n_ready"], g + 1)
                turn_group("turn_ffn", cent, g).then_inc(S["nT_done"], 1)

            def ffn_tokens(g):
                if g == 0:
                    pe.wait_ge(s_wan, 32)
                pe.wait_ge(S["nT_ready"], g + 1)
                dst = take("ffn_tokens", g)
                mm(dst[:, 0:COLS], wattn[:], xnT[:, g], start=True, stop=False, skip_group_check=True)
                for t in range(TG):
                    ins = mm(dst[:, t * P:(t + 1) * P], xin[:, g * TG + t], ident[:], start=False,
                             stop=(t == TG - 1), skip_group_check=True)
                ins.then_inc(S["xa_done"], 1)

            def expert_up(e):
                g, t = e // TG, e % TG
                pe.wait_ge(s_fc[e], 32)
                pe.wait_ge(S["xaT_ready"], g + 1)
                dst = take("expert_up", e)
                for c in range(HC):
                    ins = mm(dst[:, c * P:(c + 1) * P], fc1[:, e, c * P:(c + 1) * P],
                             qT[:, g, t * P:(t + 1) * P], start=True, stop=True)
                ins.then_inc(S["fc1_done"], 1)

            def expert_down(e):
                t = e % TG
                pe.wait_ge(S["fgelu_ready"], e + 1)
                dst = take("expert_down", e) if t == 0 else bank_of["expert_down", e - t]
                for c in range(HC):
                    ins = mm(dst[:, t * P:(t + 1) * P], fc2[:, e, c], hid[:, e, c * P:(c + 1) * P],
                             start=(c == 0), stop=(c == HC - 1))
                ins.then_inc(S["fc2_done"], 1)

            def next_layer(g):
                if g == 0:
                    pe.wait_ge(s_bias, 16 * PARTS)
                dst = take("next_layer", g)
                mm(dst[:, 0:COLS], ones16[:], bias16[:, None, :].to_broadcast([PARTS, TG, P]),
                   start=True, stop=False, skip_group_check=True)
                pe.wait_ge(S["yT_ready"], g + 1)
                for t in range(TG):
                    ins = mm(dst[:, t * P:(t + 1) * P], kT[:, g, t * P:(t + 1) * P], wnext[:],
                             start=False, stop=(t == TG - 1), skip_group_check=True)
                ins.then_inc(S["next_done"], 1)

            return (tokens, turn_input, project_qk, project_v, scores, turn_probs, attend, turn_attn, attn_out,
                    turn_mlp, mlp_up, fold_sums, mlp_down, turn_ffn, ffn_tokens, expert_up,
                    expert_down, next_layer)

        deal_banks(pe_stages())

        @block.tensor
        def _(pe):
            for stage, n in in_order(pe_stages()):
                stage(n)

        @block.sync
        def _(sp):
            def load_pixels(g):
                for i in range(XH):
                    part = slice(i * KC // XH, (i + 1) * KC // XH)
                    if g == 0:
                        sp.dma_start(tokw[:, part], tok_wT[:, part]).then_inc(s_tokw[i], 16)
                    sp.dma_start(x_sb[:, g, part], xT[g, :, part]).then_inc(s_x[g][i], 16)

            load_pixels(0)
            sp.dma_start(row_sb[:, 0:P], rows[:, 0:P].to_broadcast([P, P])).then_inc(s_tokb, 16)
            load_pixels(1)
            sp.dma_start(col_sb[:], cols).then_inc(s_col, 16)
            sp.dma_start(qkvo[:], qkvoT).then_inc(s_qkvo, 16)
            sp.dma_start(row_sb[:, P:NROW], rows[:, P:NROW].to_broadcast([P, NROW - P])).then_inc(s_row, 16)
            for g in range(2, G):
                load_pixels(g)
            sp.dma_start(w2[:], w2T).then_inc(s_w2, 16)
            sp.dma_start(w1[:], w1T).then_inc(s_w1, 16)

            def spread_k(g):
                sp.wait_ge(s_kzero, g + 1)
                sp.wait_ge(S["kT_ready"], g + 1)
                for s in range(SUB // 2):
                    at = g * TG * NB
                    sp.dma_start(kdiag[s::SUB // 2, at:at + TG * NB, s, :],
                                 kT[s::SUB // 2, g].rearrange("p (b n) -> p b n", n=N)).then_inc(s_kdiag[g], 16)

            def store(g):
                sp.wait_ge(S["out_ready"], g + 1)
                sp.dma_start(out[g], scratch(g)).then_inc(S["stored"], 16)

            for g in range(G):
                spread_k(g)
            sp.wait_ge(s_parts, 2 * PARTS - 1)
            for i in range(PARTS):
                sp.dma_start(bias16[i:i + 1, :], parts[:, i, :]).then_inc(s_bias, 16)
            sp.dma_start(wattn[:], attnT).then_inc(s_wan, 16)
            sp.dma_start(wnext[:], nextT).then_inc(s_wan, 16)
            for e in range(TILES):
                sp.dma_start(fc1[:, e], fc1T[e]).then_inc(s_fc[e], 16)
                sp.dma_start(fc2[:, e], fc2T[e]).then_inc(s_fc[e], 16)
            for g in range(G):
                store(g)
            sp.wait_ge(S["stored"], 16 * G)

        @block.gpsimd
        def _(pool):
            def inverse_root(k, g, n, at=0):
                nc.gpsimd.tensor_tensor(rstd[:, k, g, at:at + n], var[:, k, g, at:at + n], exponent[:, 0:n],
                                        ALU.pow).then_inc(s_rstd[k], 1)

            def constants(n):
                nc.gpsimd.memset(exponent[:], -0.5).then_inc(s_half, 1)
                nc.gpsimd.memset(ident[:], 0.0).then_inc(s_ident0, 1)
                pool.wait_ge(s_ident0, 1)
                nc.gpsimd.affine_select(out=ident[:], in_=ident[:], compare_op=ALU.not_equal, fill=1.0, base=0,
                                        pattern=[[-1, P]], channel_multiplier=1).then_inc(s_ident, 1)
                nc.gpsimd.memset(ones16[:], 1.0).then_inc(s_ones, 1)
                nc.gpsimd.memset(ones[:], 1.0).then_inc(s_ones, 1)
                nc.gpsimd.memset(w2n[:, :, P:P + 1], 1.0).then_inc(s_ones, 1)
                pool.wait_ge(s_half, 1)

            def clear_k(g):
                at = g * TG * NB
                nc.gpsimd.memset(kdiag[:, at:at + TG * NB], 0.0).then_inc(s_kzero, 1)

            def clear_v(n):
                nc.gpsimd.memset(vdiag[:], 0.0).then_inc(s_vzero, 1)
                pool.wait_ge(s_vzero, 1)
                for j in range(2):
                    nc.gpsimd.memset(vdiag[j * N:(j + 1) * N, :, :, j, 2 * HD:VC], 1.0).then_inc(s_ones, 1)
                    pool.wait_ge(s_ones, j + 4)

            def split_row(n):
                pool.wait_ge(s_row, 16)
                left = row("next_b")[0:1]
                for i in range(PARTS):
                    nc.gpsimd.tensor_copy(parts[:, i], left).then_inc(s_parts, 1)
                    if i < PARTS - 1:
                        pool.wait_ge(s_parts, 2 * i + 1)
                        nc.gpsimd.tensor_tensor(rest[:, i], left, parts[:, i], ALU.subtract).then_inc(s_parts, 1)
                        pool.wait_ge(s_parts, 2 * i + 2)
                        left = rest[:, i]

            def skip_input(g):
                pool.wait_ge(s_rstd[0], g + 1)
                for t in range(TG):
                    nc.gpsimd.tensor_scalar(of_group(xin, g)[:, t], of_group(h0, g)[:, t], mv[:, 0, g, t, 0:1],
                                            rstd[:, 0, g, t:t + 1], ALU.subtract, ALU.mult)\
                      .then_inc(S["xin_ready"], 1)
                if g == 0:
                    pool.wait_ge(s_row, 16)
                pool.wait_ge(S["xin_ready"], 3 * g + 2)
                nc.gpsimd.tensor_tensor(of_group(xin, g), of_group(xin, g), over_tiles(row("n2_b")), ALU.add)\
                  .then_inc(S["xin_ready"], 1)

            def root0(g):
                pool.wait_ge(s_var[0], g + 1)
                inverse_root(0, g, 2 * TG)

            def root1(t):
                pool.wait_ge(s_var[1], t + 1)
                inverse_root(1, t // TG, HEADS, (t % TG) * HEADS)

            def root2(g):
                pool.wait_ge(s_var[2], g + 1)
                inverse_root(2, g, TG)

            def root3(g):
                pool.wait_ge(s_var[3], g + 1)
                inverse_root(3, g, TG)

            def root4(g):
                pool.wait_ge(s_var[4], g + 1)
                inverse_root(4, g, TG)

            def root5(g):
                pool.wait_ge(s_var[5], g + 1)
                inverse_root(5, g, 2 * TG)

            def sums(g):
                pool.wait_ge(s_w2rows, 1)
                pool.wait_ge(S["h_ready"], g + 1)
                nc.gpsimd.tensor_tensor(of_group(hsum, g), of_group(h0, g), of_group(h, g), ALU.add)\
                  .then_inc(S["hsum_ready"], 1)
                pool.wait_ge(S["hsum_ready"], 2 * g + 1)
                nc.gpsimd.tensor_tensor(of_group(hsum, g), of_group(hsum, g), over_tiles(mlp_row[:]), ALU.add)\
                  .then_inc(S["hsum_ready"], 1)

            for stage, n in in_order((constants, clear_k, clear_v, split_row, skip_input, root0, root1, root2,
                                      root3, root4, root5, sums)):
                stage(n)

        @block.scalar
        def _(act):
            act.wait_ge(s_col, 16)
            nc.scalar.activation(sub_scale[:], col("subln_w"), ACT.Copy, scale=1.0 - LAMBDA_INIT)\
              .then_inc(s_subs, 1)

            def affine(dst, src, w, b):
                return nc.scalar.activation(dst, src, ACT.Identity, scale=w, bias=b)

            def lam_exps(n):
                act.wait_ge(s_lamdot, 1)
                nc.scalar.activation(lam_exp[:], lam_dot[:], ACT.Exp).then_inc(s_lamexp, 1)

            def input_affine(g):
                act.wait_ge(S["xcT_done"], g + 1)
                affine(xnT[:, g], bank_of["turn_input", g][:, 0:COLS], col("n1_w"), col("n1_b"))\
                    .then_inc(S["xnT_ready"], 1)

            def qk_out(g):
                act.wait_ge(S["qk_done"], g + 1)
                src = bank_of["project_qk", g]
                nc.scalar.activation(kT[:, g], src[:, COLS:2 * COLS], ACT.Copy).then_inc(S["kT_ready"], 1)
                nc.scalar.activation(qT[:, g], src[:, 0:COLS], ACT.Copy, scale=HD ** -0.5)\
                  .then_inc(S["qT_ready"], 1)

            def values(g):
                if g == 0:
                    act.wait_ge(s_vzero, 1)
                act.wait_ge(S["v_done"], g + 1)
                src = bank_of["project_v", g][:].rearrange("p (b h d) -> p b h d", h=HEADS, d=2 * HD)
                at = g * TG * NB
                for j in range(2):
                    half = slice(j * N, (j + 1) * N)
                    ins = nc.scalar.activation(vdiag[half, at:at + TG * NB, :, j, 0:2 * HD], src[half], ACT.Copy)
                ins.then_inc(S["vdiag_ready"], 1)

            def exponentials(t):
                act.wait_ge(S["shifted"], t + 1)
                nc.scalar.activation(prob[:, t % 2], prob[:, t % 2], ACT.Exp).then_inc(S["exp_done"], 1)

            def probs_out(t):
                act.wait_ge(S["probT_done"], t + 1)
                if t >= 2:
                    act.wait_ge(S["o_done"], t - 1)
                nc.scalar.activation(probT[:, t % 2], turned_ps[:], ACT.Copy).then_inc(S["probT_ready"], 1)

            def attn_square(t):
                act.wait_ge(S["attn_ready"], t + 1)
                nc.scalar.activation(squares(t), attn(t).rearrange("p h d -> p (h d)"), ACT.Square)\
                  .then_inc(S["squared"], 1)

            def attn_affine(g):
                if g == 0:
                    act.wait_ge(s_subs, 1)
                act.wait_ge(S["aT_done"], g + 1)
                nc.scalar.activation(xnT[:, g], bank_of["turn_attn", g][:, 0:COLS], ACT.Copy,
                                     scale=sub_scale[:]).then_inc(S["aT_ready"], 1)

            def mlp_affine(g):
                act.wait_ge(S["zcT_done"], g + 1)
                affine(qT[:, g], bank_of["turn_mlp", g][:, 0:COLS], col("mln1_w"), col("mln1_b"))\
                    .then_inc(S["zT_ready"], 1)

            def mlp_gelu(n):
                act.wait_ge(S["w1_done"], n + 1)
                for c in range(2):
                    chunk = 2 * (n % 2) + c
                    ins = nc.scalar.activation(hidT[:, n // 2, chunk],
                                               bank_of["mlp_up", n][:, c * COLS:(c + 1) * COLS], ACT.Gelu,
                                               bias=col("mb1", chunk))
                ins.then_inc(S["gelu_ready"], 1)

            def hidden_square(n):
                act.wait_ge(S["gelu_ready"], n + 1)
                at = 2 * (n % 2)
                nc.scalar.activation(hid[:, n].rearrange("p (c n) -> p c n", n=COLS), hidT[:, n // 2, at:at + 2],
                                     ACT.Square).then_inc(S["zsq_ready"], 1)

            def ffn_affine(g):
                act.wait_ge(S["nT_done"], g + 1)
                affine(xnT[:, g], bank_of["turn_ffn", g][:, 0:COLS], col("ln_g"), col("ln_b"))\
                    .then_inc(S["nT_ready"], 1)

            def ffn_tokens_out(g):
                act.wait_ge(S["xa_done"], g + 1)
                nc.scalar.activation(qT[:, g], bank_of["ffn_tokens", g][:, 0:COLS], ACT.Identity,
                                     bias=col("attn_b")).then_inc(S["xaT_ready"], 1)

            def expert_gelu(e):
                act.wait_ge(S["fc1_done"], e + 1)
                for c in range(HC):
                    part = slice(c * P, (c + 1) * P)
                    ins = nc.scalar.activation(hid[:, e, part], bank_of["expert_up", e][:, part], ACT.Gelu,
                                               bias=col("fc1_b", e * HC + c))
                ins.then_inc(S["fgelu_ready"], 1)

            def last_gelu(g):
                act.wait_ge(S["next_done"], g + 1)
                nc.scalar.activation(scratch(g), tiled(bank_of["next_layer", g]), ACT.Gelu)\
                  .then_inc(S["ngelu_ready"], 1)

            for stage, n in in_order((lam_exps, input_affine, qk_out, values, exponentials, probs_out, attn_square,
                                      attn_affine, mlp_affine, mlp_gelu, hidden_square, ffn_affine, ffn_tokens_out, expert_gelu,
                                      last_gelu)):
                stage(n)

        @block.vector
        def _(dve):
            steps = [0]

            def step(ins):
                steps[0] += 1
                ins.then_inc(s_dve, 1)
                return steps[0]

            def settle():
                dve.wait_ge(s_dve, steps[0])

            def moments(k, g, src):
                for t in range(TG):
                    step(nc.vector.bn_stats(stats[:, k, t], src[:, t]))
                settle()
                for t in range(TG):
                    step(nc.vector.bn_aggr(mv[:, k, g, t], stats[:, k, t]))
                settle()

            def shifted_variance(k, norm, g):
                nc.vector.tensor_scalar(var[:, norm, g, 0:TG], mv[:, k, g, :, 1], EPS, None, ALU.add)\
                  .then_inc(s_var[norm], 1)

            def double_variance(k, norm, g):
                step(nc.vector.tensor_scalar(var[:, norm, g, TG:2 * TG], mv[:, k, g, :, 1], 1.0 + EPS, EPS * EPS,
                                             ALU.mult, ALU.add))
                nc.vector.tensor_scalar(var[:, norm, g, 0:TG], mv[:, k, g, :, 1], EPS, None, ALU.add)\
                  .then_inc(s_var[norm], 1)

            def normalise(dst, src, k, norm, g, second=0):
                for t in range(TG):
                    ins = nc.vector.tensor_scalar(dst[:, t], src[:, t], mv[:, k, g, t, 0:1],
                                                  rstd[:, norm, g, second * TG + t:second * TG + t + 1],
                                                  ALU.subtract, ALU.mult)
                return ins

            def add(dst, a, b):
                return nc.vector.tensor_tensor(dst, a, b, ALU.add)

            def lam_dots(n):
                dve.wait_ge(s_row, 16)
                q1k1q2k2 = row("lam").rearrange("p (a b d) -> p a b d", a=2, b=2)
                step(nc.vector.tensor_tensor(lam_prod[:], q1k1q2k2[:, :, 0], q1k1q2k2[:, :, 1], ALU.mult))
                settle()
                nc.vector.tensor_reduce(lam_dot[:], lam_prod[:], AX, ALU.add).then_inc(s_lamdot, 1)

            def lam(n):
                dve.wait_ge(s_lamexp, 1)
                step(nc.vector.tensor_tensor(lam_diff[:], lam_exp[:, 1:2], lam_exp[:, 0:1], ALU.subtract))
                settle()
                step(nc.vector.tensor_scalar(neg_lam[:], lam_diff[:], -LAMBDA_INIT, None, ALU.add))

            def fold_weights(n):
                dve.wait_ge(s_w2, 16)
                dve.wait_ge(s_col, 16)
                at = COL["mln2_w"][0]
                nc.vector.tensor_tensor(w2n[:, :, 0:P], w2[:], col_sb[:, at:at + HC][:, :, None].to_broadcast([P, HC, P]),
                                        ALU.mult)
                at = COL["mln2_b"][0]
                nc.vector.tensor_copy(mln2_b[:], col_sb[:, at:at + HC][:, :, None].to_broadcast([P, HC, P]))\
                  .then_inc(s_w2n, 1)

            def fold_rows(n):
                dve.wait_ge(s_w2sums, 1)
                dve.wait_ge(s_row, 16)
                src = bank_of["fold_sums", 0]
                step(nc.vector.tensor_copy(w2n_sums[:], src[:, 0:P]))
                add(mlp_row[:], src[:, P:2 * P], row("mb2")).then_inc(s_w2rows, 1)

            def embedding(g):
                if g == 0:
                    dve.wait_ge(s_tokb, 16)
                dve.wait_ge(S["tok_done"], g + 1)
                add(of_group(h0, g), tiled(bank_of["tokens", g]), over_tiles(row("tok_b")))\
                    .then_inc(S["h0_ready"], 1)
                dve.wait_ge(S["h0_ready"], g + 1)
                moments(0, g, of_group(h0, g))
                double_variance(0, 0, g)

            def input_norm(g):
                dve.wait_ge(s_rstd[0], g + 1)
                normalise(of_group(cent, g), of_group(h0, g), 0, 0, g, second=1).then_inc(S["xc_ready"], 1)

            def softmax_shift(t):
                dve.wait_ge(S["s_done"], t + 1)
                step(nc.vector.tensor_reduce(negmax[:, t % 2], score_ps[:], AX, ALU.max, negate=True))
                settle()
                if t >= 2:
                    dve.wait_ge(S["probT_done"], t - 1)
                add(prob[:, t % 2], score_ps[:], negmax[:, t % 2][:, :, None].to_broadcast([P, SUB, N]))\
                    .then_inc(S["shifted"], 1)

            def difference(t):
                dve.wait_ge(S["o_done"], t + 1)
                step(nc.vector.reciprocal(rden[:, t % 2], value_ps[:, :, :, 2 * HD]))
                settle()
                step(nc.vector.tensor_scalar(rden[:, t % 2, :, 1], rden[:, t % 2, :, 1], neg_lam[:], None, ALU.mult))
                settle()
                nc.vector.tensor_tensor(onorm[:, t % 2], value_ps[:, :, :, 0:2 * HD],
                                        rden[:, t % 2][:, :, :, None].to_broadcast([P, HEADS, 2, 2 * HD]),
                                        ALU.mult).then_inc(S["o_read"], 1)
                dve.wait_ge(S["o_read"], t + 1)
                add(attn(t), onorm[:, t % 2, :, 0], onorm[:, t % 2, :, 1]).then_inc(S["attn_ready"], 1)

            def rms(t):
                dve.wait_ge(S["squared"], t + 1)
                mine = var[:, 1, t // TG, (t % TG) * HEADS:(t % TG + 1) * HEADS]
                step(nc.vector.tensor_reduce(mine, squares(t).rearrange("p (h d) -> p h d", d=2 * HD), AX, ALU.add))
                settle()
                nc.vector.tensor_scalar(mine, mine, 1.0 / (2 * HD), EPS, ALU.mult, ALU.add).then_inc(s_var[1], 1)

            def rms_apply(t):
                dve.wait_ge(s_rstd[1], t + 1)
                mine = rstd[:, 1, t // TG, (t % TG) * HEADS:(t % TG + 1) * HEADS]
                nc.vector.tensor_tensor(cent[:, t].rearrange("p (h d) -> p h d", d=2 * HD), attn(t),
                                        mine[:, :, None].to_broadcast([P, HEADS, 2 * HD]), ALU.mult)\
                  .then_inc(S["rms_ready"], 1)

            def second_moments(g):
                dve.wait_ge(S["wo_done"], g + 1)
                moments(1, g, tiled(bank_of["attn_out", g]))
                shifted_variance(1, 2, g)

            def residual(g):
                dve.wait_ge(s_rstd[2], g + 1)
                if g == 0:
                    dve.wait_ge(s_row, 16)
                src = tiled(bank_of["attn_out", g])
                for t in range(TG):
                    step(nc.vector.scalar_tensor_tensor(scratch(g)[:, t], src[:, t], mv[:, 1, g, t, 0:1],
                                                        row("n2_w"), ALU.subtract, ALU.mult))
                settle()
                dve.wait_ge(S["xin_ready"], 3 * (g + 1))
                for t in range(TG):
                    ins = nc.vector.scalar_tensor_tensor(of_group(h, g)[:, t], scratch(g)[:, t],
                                                         rstd[:, 2, g, t:t + 1], of_group(xin, g)[:, t],
                                                         ALU.mult, ALU.add)
                ins.then_inc(S["h_ready"], 1)
                dve.wait_ge(S["h_ready"], g + 1)
                moments(2, g, of_group(h, g))
                shifted_variance(2, 3, g)

            def mlp_norm(g):
                dve.wait_ge(s_rstd[3], g + 1)
                normalise(of_group(cent, g), of_group(h, g), 2, 3, g).then_inc(S["zc_ready"], 1)

            def sum_squares(g):
                dve.wait_ge(S["zsq_ready"], 2 * (g + 1))
                nc.vector.tensor_reduce(square_sums(g),
                                        of_group(hid, g).rearrange("p t (c n) -> p n (t c)", n=COLS), AX, ALU.add)\
                  .then_inc(S["sumsq_ready"], 1)

            def hidden_stats(g):
                dve.wait_ge(S["w2_done"], g + 1)
                src = bank_of["mlp_down", g]
                mean, second = mv[:, 3, g, :, 0], mv[:, 3, g, :, 1]
                step(nc.vector.tensor_scalar(mean, src[:, 0:TG * (P + 1)].rearrange("p (t n) -> p t n", t=TG)[:, :, P],
                                             1.0 / HID, None, ALU.mult))
                settle()
                step(nc.vector.scalar_tensor_tensor(mean_sq[:], mean, 1.0, mean, ALU.mult, ALU.mult))
                settle()
                step(nc.vector.scalar_tensor_tensor(second, src[:, TG * (P + 1):TG * (P + 1) + TG], 1.0 / HID, mean_sq[:],
                                                    ALU.mult, ALU.subtract))
                settle()
                nc.vector.tensor_scalar(var[:, 4, g, 0:TG], second, 0.0, EPS, ALU.max, ALU.add)\
                  .then_inc(s_var[4], 1)

            def mlp_result(g):
                dve.wait_ge(s_rstd[4], g + 1)
                step(nc.vector.scalar_tensor_tensor(nmr[:, g], mv[:, 3, g, :, 0], -1.0, rstd[:, 4, g, 0:TG],
                                                    ALU.mult, ALU.mult))
                settle()
                dve.wait_ge(S["hsum_ready"], 2 * (g + 1))
                for t in range(TG):
                    step(nc.vector.scalar_tensor_tensor(of_group(hsum, g)[:, t], w2n_sums[:], nmr[:, g, t:t + 1],
                                                        of_group(hsum, g)[:, t], ALU.mult, ALU.add))
                settle()
                dve.wait_ge(S["w2_done"], g + 1)
                src = bank_of["mlp_down", g][:, 0:TG * (P + 1)].rearrange("p (t n) -> p t n", t=TG)[:, :, 0:P]
                for t in range(TG):
                    ins = nc.vector.scalar_tensor_tensor(of_group(h1, g)[:, t], src[:, t], rstd[:, 4, g, t:t + 1],
                                                         of_group(hsum, g)[:, t], ALU.mult, ALU.add)
                ins.then_inc(S["h1_ready"], 1)
                dve.wait_ge(S["h1_ready"], g + 1)
                moments(4, g, of_group(h1, g))
                double_variance(4, 5, g)

            def ffn_norm(g):
                dve.wait_ge(s_rstd[5], g + 1)
                normalise(of_group(cent, g), of_group(h1, g), 4, 5, g, second=1)
                normalise(of_group(xin, g), of_group(h1, g), 4, 5, g).then_inc(S["n_ready"], 1)

            def expert_out(g):
                dve.wait_ge(S["fc2_done"], (g + 1) * TG)
                at = COL["fc2_b"][0] + g * TG
                add(tiled(kT[:, g]), tiled(bank_of["expert_down", g * TG]),
                    col_sb[:, at:at + TG][:, :, None].to_broadcast([P, TG, P])).then_inc(S["yT_ready"], 1)

            def output(g):
                dve.wait_ge(S["ngelu_ready"], g + 1)
                add(scratch(g), scratch(g), of_group(h1, g)).then_inc(S["out_ready"], 1)

            for stage, n in in_order((lam_dots, lam, fold_weights, fold_rows, embedding, input_norm,
                                      softmax_shift, difference, rms, rms_apply, second_moments, residual, mlp_norm,
                                      sum_squares, hidden_stats, mlp_result, ffn_norm, expert_out, output)):
                stage(n)


def kernel(x, L0_tok_w, L0_tok_b, L0_attn_Wq, L0_attn_Wk, L0_attn_Wv, L0_attn_Wo, L0_attn_lq1, L0_attn_lk1,
           L0_attn_lq2, L0_attn_lk2, L0_attn_subln_w, L0_attn_n1_w, L0_attn_n1_b, L0_attn_n2_w, L0_attn_n2_b,
           L0_attn_mln1_w, L0_attn_mln1_b, L0_attn_mW1, L0_attn_mb1, L0_attn_mln2_w, L0_attn_mln2_b, L0_attn_mW2,
           L0_attn_mb2, L0_ffn_ln_g, L0_ffn_ln_b, L0_ffn_attn_w, L0_ffn_attn_b, L0_ffn_gate_w, L0_ffn_fc1_w,
           L0_ffn_fc1_b, L0_ffn_fc2_w, L0_ffn_fc2_b, L0_ffn_next_w, L0_ffn_next_b):
    import numpy as np
    import concourse.bacc as bacc
    from concourse.bass_utils import run_bass_kernel_spmd

    def vectors(a):
        return np.asarray(a).reshape(-1, P).T

    def maps_last(w):
        return np.asarray(w).reshape(2, SUB // 2, HD, P).transpose(3, 0, 2, 1).reshape(P, P)

    side = np.asarray(x).shape[2] // 16
    px = np.asarray(x).reshape(NB, G, TG, 3, side, 16, side, 16).transpose(3, 5, 7, 1, 2, 0, 4, 6)
    px = px.reshape(KC, P, G, COLS).transpose(2, 1, 0, 3)
    columns = {"n1_w": L0_attn_n1_w, "n1_b": L0_attn_n1_b, "subln_w": np.tile(np.asarray(L0_attn_subln_w), HEADS),
               "mln1_w": L0_attn_mln1_w, "mln1_b": L0_attn_mln1_b, "mb1": L0_attn_mb1, "mln2_w": L0_attn_mln2_w,
               "mln2_b": L0_attn_mln2_b, "ln_g": L0_ffn_ln_g, "ln_b": L0_ffn_ln_b, "attn_b": L0_ffn_attn_b,
               "fc1_b": L0_ffn_fc1_b, "fc2_b": L0_ffn_fc2_b}
    lam = np.concatenate([np.asarray(v) for v in (L0_attn_lq1, L0_attn_lk1, L0_attn_lq2, L0_attn_lk2)])
    rows = {"tok_b": L0_tok_b, "n2_w": L0_attn_n2_w, "n2_b": L0_attn_n2_b, "mb2": L0_attn_mb2,
            "lam": lam, "next_b": L0_ffn_next_b}
    arrays = {
        "xT": px,
        "tok_wT": np.asarray(L0_tok_w).T.reshape(KC, P, P).transpose(1, 0, 2),
        "cols": np.concatenate([vectors(columns[n]) for n in COL], axis=1),
        "rows": np.concatenate([np.asarray(rows[n]).reshape(1, -1) for n in ROW], axis=1),
        "qkvoT": np.stack([maps_last(L0_attn_Wq), maps_last(L0_attn_Wk), np.asarray(L0_attn_Wv).T,
                           np.asarray(L0_attn_Wo).T], axis=1),
        "w1T": np.asarray(L0_attn_mW1).T,
        "w2T": np.asarray(L0_attn_mW2).T.reshape(HC, P, P).transpose(1, 0, 2),
        "attnT": np.asarray(L0_ffn_attn_w).T,
        "nextT": np.asarray(L0_ffn_next_w).T,
        "fc1T": np.asarray(L0_ffn_fc1_w).transpose(0, 2, 1),
        "fc2T": np.asarray(L0_ffn_fc2_w).transpose(0, 2, 1).reshape(TILES, HC, P, P).transpose(0, 2, 1, 3),
    }
    arrays = {k: np.ascontiguousarray(v) for k, v in arrays.items()}
    nc = bacc.Bacc("TRN2", target_bir_lowering=False, num_devices=1)
    args = [nc.dram_tensor(n, a.shape, mybir.dt.from_np(a.dtype), kind="ExternalInput").ap() for n, a in arrays.items()]
    out = nc.dram_tensor("out", (G, P, TG, P), mybir.dt.float32, kind="ExternalOutput").ap()
    vit_layer(nc, *args, out)
    r = run_bass_kernel_spmd(nc, [arrays], core_ids=[0])
    y = r.results[0]["out"].reshape(G, NB, N, TG, P).transpose(1, 0, 3, 2, 4)
    return np.ascontiguousarray(y.reshape(NB * G * TG, N, P))
```
